# Optimizing a Trainium2 kernel written in Bass

```python
import numpy as np
import jax
import jax.numpy as jnp

def _softmax(x, axis=-1):
    return jax.nn.softmax(x, axis=axis)

def _gelu(x):
    return jax.nn.gelu(x, approximate=True)

def _silu(x):
    return jax.nn.silu(x)

def _sigmoid(x):
    return jax.nn.sigmoid(x)

def _layernorm(x, axis=-1, eps=1e-05):
    m = jnp.mean(x, axis=axis, keepdims=True)
    v = jnp.var(x, axis=axis, keepdims=True)
    return (x - m) / jnp.sqrt(v + eps)

def _scatter_add(tgt, idx, src, axis=0):
    return tgt.at[idx].add(src)

def _segment_sum(src, seg, n):
    return jax.ops.segment_sum(src, seg, n)
kernel_name = 'mk_adaln_d2_jaxref_r4_95a7eb'

def setup_inputs(seed: int=0):
    np.random.seed(seed)
    _w = jnp.asarray

    def _L0_attn_setup():
        import jax, jax.numpy as jnp
        import numpy as np
        import math
        EMBED_DIM = 512
        N_HEADS = 16
        HEAD_DIM = EMBED_DIM // N_HEADS
        THETA_BASE = 10000.0

        def _rope_freqs(seq_len):
            i = jnp.arange(HEAD_DIM // 2, dtype=jnp.float32)
            inv_freq = 1.0 / THETA_BASE ** (2.0 * i / HEAD_DIM)
            pos = jnp.arange(seq_len, dtype=jnp.float32)
            th = jnp.outer(pos, inv_freq)
            return (jnp.cos(th), jnp.sin(th))

        def _rope(t, cos, sin):
            b, h, s, d = t.shape
            tr = t.reshape(b, h, s, d // 2, 2)
            x0, x1 = (tr[..., 0], tr[..., 1])
            r0 = x0 * cos - x1 * sin
            r1 = x0 * sin + x1 * cos
            return jnp.stack([r0, r1], axis=-1).reshape(b, h, s, d)
        key = jax.random.key(seed)
        k1, k2, k3 = jax.random.split(key, 3)
        B, S = (2, 512)
        x = jax.random.normal(k1, (B, S, EMBED_DIM), jnp.float32)
        scale = EMBED_DIM ** (-0.5)
        Wqkv = jax.random.normal(k2, (EMBED_DIM, 3 * EMBED_DIM), jnp.float32) * scale
        Wo = jax.random.normal(k3, (EMBED_DIM, EMBED_DIM), jnp.float32) * scale
        return {'x': x, 'Wqkv': Wqkv, 'Wo': Wo}
    _L0_attn_in = _L0_attn_setup()

    def _L0_ffn_setup():
        import jax, jax.numpy as jnp
        import numpy as np
        B, S, H = (2, 256, 512)
        E, K = (8, 2)
        F = 352
        FS = 1408
        NORM_TOPK = False

        def _swiglu(x, wg, wu, wd):
            return jax.nn.silu(x @ wg) * (x @ wu) @ wd
        key = jax.random.key(seed)
        ks = jax.random.split(key, 9)
        s = 0.02
        return {'hidden_states': jax.random.normal(ks[0], (B, S, H), dtype=jnp.float32), 'Wr': jax.random.normal(ks[1], (H, E), dtype=jnp.float32) * s, 'Wg': jax.random.normal(ks[2], (E, H, F), dtype=jnp.float32) * s, 'Wu': jax.random.normal(ks[3], (E, H, F), dtype=jnp.float32) * s, 'Wd': jax.random.normal(ks[4], (E, F, H), dtype=jnp.float32) * s, 'Sg': jax.random.normal(ks[5], (H, FS), dtype=jnp.float32) * s, 'Su': jax.random.normal(ks[6], (H, FS), dtype=jnp.float32) * s, 'Sd': jax.random.normal(ks[7], (FS, H), dtype=jnp.float32) * s, 'Wsg': jax.random.normal(ks[8], (H, 1), dtype=jnp.float32) * s}
    _L0_ffn_in = _L0_ffn_setup()
    _L0_c = _w((lambda *s: np.random.randn(*s).astype(np.float32) * 0.05)(1, 512))
    _L0_wmod = _w((lambda *s: np.random.randn(*s).astype(np.float32) * 0.05)(512, 6 * 512) * 512 ** (-0.5))

    def _L1_attn_setup():
        import jax, jax.numpy as jnp
        import numpy as np
        from jax import lax
        H = 16
        D = 128
        HID = 512
        CONV_K = 4
        CHUNK = 64
        EPS = 1e-06

        def silu(x):
            return x * jax.nn.sigmoid(x)

        def short_conv(x, w):
            B, T, C = x.shape
            K = w.shape[1]
            xp = jnp.pad(x, ((0, 0), (K - 1, 0), (0, 0)))
            y = sum((xp[:, j:j + T, :] * w[None, None, :, j] for j in range(K)))
            return silu(y)

        def l2norm(x):
            return x * lax.rsqrt(jnp.sum(x * x, -1, keepdims=True) + EPS)

        def rmsnorm(x, w):
            return x * lax.rsqrt(jnp.mean(x * x, -1, keepdims=True) + EPS) * w

        def kda_scan(q, k, v, g, beta):
            B, T, _, _ = q.shape
            NC = T // CHUNK

            def tm(a):
                a = jnp.moveaxis(a, 1, 0)
                return a.reshape((NC, CHUNK) + a.shape[1:])

            def step(S, inp):
                qt, kt, vt, gt, bt = inp
                S = S * jnp.exp(gt)[..., :, None]
                u = (vt - jnp.einsum('bhk,bhkv->bhv', kt, S)) * bt[..., None]
                S = S + kt[..., None] * u[..., None, :]
                ot = jnp.einsum('bhk,bhkv->bhv', qt, S)
                return (S, ot)

            @jax.checkpoint
            def chunk_body(S, inp):
                return lax.scan(step, S, inp)
            S0 = jnp.zeros((B, H, D, D), dtype=q.dtype)
            _, o = lax.scan(chunk_body, S0, (tm(q), tm(k), tm(v), tm(g), tm(beta)))
            o = o.reshape(T, B, H, D)
            return jnp.moveaxis(o, 0, 1)
        key = jax.random.key(seed)
        ks = jax.random.split(key, 16)
        s_h = 1.0 / np.sqrt(HID)
        s_d = 1.0 / np.sqrt(D)
        inp = {'hidden_states': jax.random.normal(ks[0], (2, 1024, HID), dtype=jnp.float32), 'Wq': jax.random.normal(ks[1], (HID, H * D), dtype=jnp.float32) * s_h, 'Wk': jax.random.normal(ks[2], (HID, H * D), dtype=jnp.float32) * s_h, 'Wv': jax.random.normal(ks[3], (HID, H * D), dtype=jnp.float32) * s_h, 'conv_q_w': jax.random.normal(ks[4], (H * D, CONV_K), dtype=jnp.float32) * 0.5, 'conv_k_w': jax.random.normal(ks[5], (H * D, CONV_K), dtype=jnp.float32) * 0.5, 'conv_v_w': jax.random.normal(ks[6], (H * D, CONV_K), dtype=jnp.float32) * 0.5, 'A_log': jnp.log(jax.random.uniform(ks[7], (1, 1, H, 1), dtype=jnp.float32, minval=1.0, maxval=16.0)), 'Wfa': jax.random.normal(ks[8], (HID, D), dtype=jnp.float32) * s_h, 'Wfb': jax.random.normal(ks[9], (D, H * D), dtype=jnp.float32) * s_d, 'dt_bias': jax.random.normal(ks[10], (H * D,), dtype=jnp.float32) * 0.5, 'Wb': jax.random.normal(ks[11], (HID, H), dtype=jnp.float32) * s_h, 'Wga': jax.random.normal(ks[12], (HID, D), dtype=jnp.float32) * s_h, 'Wgb': jax.random.normal(ks[13], (D, H * D), dtype=jnp.float32) * s_d, 'o_norm_w': jnp.ones((D,), dtype=jnp.float32), 'Wo': jax.random.normal(ks[14], (H * D, HID), dtype=jnp.float32) * s_h}
        return inp
    _L1_attn_in = _L1_attn_setup()

    def _L1_ffn_setup():
        import jax, jax.numpy as jnp
        import numpy as np

        def ternary_quantize(t, threshold, scale):
            return jnp.where(t > threshold, scale, jnp.where(t < -threshold, -scale, 0.0)).astype(t.dtype)
        key = jax.random.key(seed)
        k1, k2, k3 = jax.random.split(key, 3)
        B, S, D = (4, 1024, 512)
        x = jax.random.normal(k1, (B, S, D), dtype=jnp.float32)
        weight = jax.random.normal(k2, (D, D), dtype=jnp.float32) * 0.02
        rram_variation = jax.random.normal(k3, (D, D), dtype=jnp.float32) * 0.05
        return {'x': x, 'weight': weight, 'rram_variation': rram_variation}
    _L1_ffn_in = _L1_ffn_setup()
    _L1_c = _w((lambda *s: np.random.randn(*s).astype(np.float32) * 0.05)(1, 512))
    _L1_wmod = _w((lambda *s: np.random.randn(*s).astype(np.float32) * 0.05)(512, 6 * 512) * 512 ** (-0.5))
    _d = {'L0_attn_x': _L0_attn_in['x'], 'L0_attn_Wqkv': _L0_attn_in['Wqkv'], 'L0_attn_Wo': _L0_attn_in['Wo'], 'L0_ffn_Wr': _L0_ffn_in['Wr'], 'L0_ffn_Wg': _L0_ffn_in['Wg'], 'L0_ffn_Wu': _L0_ffn_in['Wu'], 'L0_ffn_Wd': _L0_ffn_in['Wd'], 'L0_ffn_Sg': _L0_ffn_in['Sg'], 'L0_ffn_Su': _L0_ffn_in['Su'], 'L0_ffn_Sd': _L0_ffn_in['Sd'], 'L0_ffn_Wsg': _L0_ffn_in['Wsg'], 'L0_c': _L0_c, 'L0_wmod': _L0_wmod, 'L1_attn_Wq': _L1_attn_in['Wq'], 'L1_attn_Wk': _L1_attn_in['Wk'], 'L1_attn_Wv': _L1_attn_in['Wv'], 'L1_attn_conv_q_w': _L1_attn_in['conv_q_w'], 'L1_attn_conv_k_w': _L1_attn_in['conv_k_w'], 'L1_attn_conv_v_w': _L1_attn_in['conv_v_w'], 'L1_attn_A_log': _L1_attn_in['A_log'], 'L1_attn_Wfa': _L1_attn_in['Wfa'], 'L1_attn_Wfb': _L1_attn_in['Wfb'], 'L1_attn_dt_bias': _L1_attn_in['dt_bias'], 'L1_attn_Wb': _L1_attn_in['Wb'], 'L1_attn_Wga': _L1_attn_in['Wga'], 'L1_attn_Wgb': _L1_attn_in['Wgb'], 'L1_attn_o_norm_w': _L1_attn_in['o_norm_w'], 'L1_attn_Wo': _L1_attn_in['Wo'], 'L1_ffn_weight': _L1_ffn_in['weight'], 'L1_ffn_rram_variation': _L1_ffn_in['rram_variation'], 'L1_c': _L1_c, 'L1_wmod': _L1_wmod}
    _x0 = _d['L0_attn_x']
    _d['L0_attn_x'] = jax.random.normal(jax.random.fold_in(jax.random.key(seed), 1), (1, 2048, 512), dtype=_x0.dtype)
    del _x0
    return _d

def reference(L0_attn_x, L0_attn_Wqkv, L0_attn_Wo, L0_ffn_Wr, L0_ffn_Wg, L0_ffn_Wu, L0_ffn_Wd, L0_ffn_Sg, L0_ffn_Su, L0_ffn_Sd, L0_ffn_Wsg, L0_c, L0_wmod, L1_attn_Wq, L1_attn_Wk, L1_attn_Wv, L1_attn_conv_q_w, L1_attn_conv_k_w, L1_attn_conv_v_w, L1_attn_A_log, L1_attn_Wfa, L1_attn_Wfb, L1_attn_dt_bias, L1_attn_Wb, L1_attn_Wga, L1_attn_Wgb, L1_attn_o_norm_w, L1_attn_Wo, L1_ffn_weight, L1_ffn_rram_variation, L1_c, L1_wmod):

    def _L0_attn_ref(x, Wqkv, Wo):
        import jax, jax.numpy as jnp
        import numpy as np
        import math
        EMBED_DIM = 512
        N_HEADS = 16
        HEAD_DIM = EMBED_DIM // N_HEADS
        THETA_BASE = 10000.0

        def _rope_freqs(seq_len):
            i = jnp.arange(HEAD_DIM // 2, dtype=jnp.float32)
            inv_freq = 1.0 / THETA_BASE ** (2.0 * i / HEAD_DIM)
            pos = jnp.arange(seq_len, dtype=jnp.float32)
            th = jnp.outer(pos, inv_freq)
            return (jnp.cos(th), jnp.sin(th))

        def _rope(t, cos, sin):
            b, h, s, d = t.shape
            tr = t.reshape(b, h, s, d // 2, 2)
            x0, x1 = (tr[..., 0], tr[..., 1])
            r0 = x0 * cos - x1 * sin
            r1 = x0 * sin + x1 * cos
            return jnp.stack([r0, r1], axis=-1).reshape(b, h, s, d)
        B, S, E = x.shape
        H, D = (N_HEADS, E // N_HEADS)
        qkv = x @ Wqkv
        q, k, v = jnp.split(qkv, 3, axis=-1)
        heads = lambda t: t.reshape(B, S, H, D).transpose(0, 2, 1, 3)
        q, k, v = (heads(q), heads(k), heads(v))
        cos, sin = _rope_freqs(S)
        q = _rope(q, cos, sin)
        k = _rope(k, cos, sin)
        scores = jnp.einsum('bhqd,bhkd->bhqk', q, k) / math.sqrt(D)
        causal = jnp.tril(jnp.ones((S, S), dtype=bool))
        scores = jnp.where(causal, scores, -jnp.inf)
        attn = jax.nn.softmax(scores, axis=-1)
        op = jnp.einsum('bhqk,bhkd->bhqd', attn, v)
        op = op.transpose(0, 2, 1, 3).reshape(B, S, E)
        return op @ Wo

    def _L0_ffn_ref(hidden_states, Wr, Wg, Wu, Wd, Sg, Su, Sd, Wsg):
        import jax, jax.numpy as jnp
        import numpy as np
        B, S, H = (2, 256, 512)
        E, K = (8, 2)
        F = 352
        FS = 1408
        NORM_TOPK = False

        def _swiglu(x, wg, wu, wd):
            return jax.nn.silu(x @ wg) * (x @ wu) @ wd
        b, s, h = hidden_states.shape
        x = hidden_states.reshape(-1, h)
        router_logits = x @ Wr
        probs = jax.nn.softmax(router_logits.astype(jnp.float32), axis=-1)
        routing_weights, selected = jax.lax.top_k(probs, K)
        if NORM_TOPK:
            routing_weights = routing_weights / routing_weights.sum(-1, keepdims=True)
        routing_weights = routing_weights.astype(x.dtype)
        C = jnp.einsum('tk,tke->te', routing_weights, jax.nn.one_hot(selected, E, dtype=x.dtype))
        expert_out = jax.vmap(lambda wg, wu, wd: _swiglu(x, wg, wu, wd))(Wg, Wu, Wd)
        moe_out = jnp.einsum('te,eth->th', C, expert_out)
        shared = _swiglu(x, Sg, Su, Sd)
        shared = jax.nn.sigmoid(x @ Wsg) * shared
        out = (moe_out + shared).reshape(b, s, h)
        return out

    def _L1_attn_ref(hidden_states, Wq, Wk, Wv, conv_q_w, conv_k_w, conv_v_w, A_log, Wfa, Wfb, dt_bias, Wb, Wga, Wgb, o_norm_w, Wo):
        import jax, jax.numpy as jnp
        import numpy as np
        from jax import lax
        H = 16
        D = 128
        HID = 512
        CONV_K = 4
        CHUNK = 64
        EPS = 1e-06

        def silu(x):
            return x * jax.nn.sigmoid(x)

        def short_conv(x, w):
            B, T, C = x.shape
            K = w.shape[1]
            xp = jnp.pad(x, ((0, 0), (K - 1, 0), (0, 0)))
            y = sum((xp[:, j:j + T, :] * w[None, None, :, j] for j in range(K)))
            return silu(y)

        def l2norm(x):
            return x * lax.rsqrt(jnp.sum(x * x, -1, keepdims=True) + EPS)

        def rmsnorm(x, w):
            return x * lax.rsqrt(jnp.mean(x * x, -1, keepdims=True) + EPS) * w

        def kda_scan(q, k, v, g, beta):
            B, T, _, _ = q.shape
            NC = T // CHUNK

            def tm(a):
                a = jnp.moveaxis(a, 1, 0)
                return a.reshape((NC, CHUNK) + a.shape[1:])

            def step(S, inp):
                qt, kt, vt, gt, bt = inp
                S = S * jnp.exp(gt)[..., :, None]
                u = (vt - jnp.einsum('bhk,bhkv->bhv', kt, S)) * bt[..., None]
                S = S + kt[..., None] * u[..., None, :]
                ot = jnp.einsum('bhk,bhkv->bhv', qt, S)
                return (S, ot)

            @jax.checkpoint
            def chunk_body(S, inp):
                return lax.scan(step, S, inp)
            S0 = jnp.zeros((B, H, D, D), dtype=q.dtype)
            _, o = lax.scan(chunk_body, S0, (tm(q), tm(k), tm(v), tm(g), tm(beta)))
            o = o.reshape(T, B, H, D)
            return jnp.moveaxis(o, 0, 1)
        B, T, _ = hidden_states.shape
        q = short_conv(hidden_states @ Wq, conv_q_w)
        k = short_conv(hidden_states @ Wk, conv_k_w)
        v = short_conv(hidden_states @ Wv, conv_v_w)
        g = (hidden_states @ Wfa @ Wfb).reshape(B, T, H, D)
        g = -jnp.exp(A_log) * jax.nn.softplus(g + dt_bias.reshape(1, 1, H, D))
        beta = jax.nn.sigmoid(hidden_states @ Wb)
        q = l2norm(q.reshape(B, T, H, D)) * D ** (-0.5)
        k = l2norm(k.reshape(B, T, H, D))
        v = v.reshape(B, T, H, D)
        o = kda_scan(q, k, v, g, beta)
        go = (hidden_states @ Wga @ Wgb).reshape(B, T, H, D)
        o = rmsnorm(o, o_norm_w) * jax.nn.sigmoid(go)
        o = o.reshape(B, T, H * D) @ Wo
        return o

    def _L1_ffn_ref(x, weight, rram_variation):
        import jax, jax.numpy as jnp
        import numpy as np

        def ternary_quantize(t, threshold, scale):
            return jnp.where(t > threshold, scale, jnp.where(t < -threshold, -scale, 0.0)).astype(t.dtype)
        TH_X, SC_X = (0.33, 0.5)
        TH_W, SC_W = (0.2, 0.6)
        x_q = ternary_quantize(x, TH_X, SC_X)
        w_q = ternary_quantize(weight, TH_W, SC_W)
        w_rram = w_q + rram_variation
        return jnp.einsum('bsd,od->bso', x_q, w_rram)
    x = L0_attn_x
    mod = (_silu(L0_c) @ L0_wmod).reshape(L0_c.shape[0], 6, 1, -1)
    sa, ca, ga, sb, cb, gb = (mod[:, 0], mod[:, 1], mod[:, 2], mod[:, 3], mod[:, 4], mod[:, 5])
    ga = (2 * (ga >= 0) - 1) * jnp.maximum(jnp.abs(ga), 0.25)
    gb = (2 * (gb >= 0) - 1) * jnp.maximum(jnp.abs(gb), 0.25)
    h = _layernorm(x, axis=-1) * (1 + ca) + sa
    x = x + ga * _L0_attn_ref(h, L0_attn_Wqkv, L0_attn_Wo)
    h = _layernorm(x, axis=-1) * (1 + cb) + sb
    x = x + gb * _L0_ffn_ref(h, L0_ffn_Wr, L0_ffn_Wg, L0_ffn_Wu, L0_ffn_Wd, L0_ffn_Sg, L0_ffn_Su, L0_ffn_Sd, L0_ffn_Wsg)
    mod = (_silu(L1_c) @ L1_wmod).reshape(L1_c.shape[0], 6, 1, -1)
    sa, ca, ga, sb, cb, gb = (mod[:, 0], mod[:, 1], mod[:, 2], mod[:, 3], mod[:, 4], mod[:, 5])
    ga = (2 * (ga >= 0) - 1) * jnp.maximum(jnp.abs(ga), 0.25)
    gb = (2 * (gb >= 0) - 1) * jnp.maximum(jnp.abs(gb), 0.25)
    h = _layernorm(x, axis=-1) * (1 + ca) + sa
    x = x + ga * _L1_attn_ref(h, L1_attn_Wq, L1_attn_Wk, L1_attn_Wv, L1_attn_conv_q_w, L1_attn_conv_k_w, L1_attn_conv_v_w, L1_attn_A_log, L1_attn_Wfa, L1_attn_Wfb, L1_attn_dt_bias, L1_attn_Wb, L1_attn_Wga, L1_attn_Wgb, L1_attn_o_norm_w, L1_attn_Wo)
    h = _layernorm(x, axis=-1) * (1 + cb) + sb
    x = x + gb * _L1_ffn_ref(h, L1_ffn_weight, L1_ffn_rram_variation)
    return x

_drawn_inputs = setup_inputs


def setup_inputs(seed=0):
    import zlib

    import numpy as np

    out = dict(_drawn_inputs(seed))
    spreads = {'L1_attn_o_norm_w': (1.0, 0.6)}
    factors = {'L0_ffn_Wr': 8.0,
     'L0_ffn_Wg': 8.0,
     'L0_ffn_Wu': 8.0,
     'L0_ffn_Wd': 8.0,
     'L0_ffn_Sg': 4.052,
     'L0_ffn_Su': 3.975,
     'L0_ffn_Sd': 3.983,
     'L0_ffn_Wsg': 8.0,
     'L1_attn_A_log': 26.512,
     'L1_attn_Wfa': 8.0,
     'L1_attn_Wfb': 8.0,
     'L1_attn_dt_bias': 37.302,
     'L1_attn_Wb': 7.533,
     'L1_attn_Wga': 3.365,
     'L1_attn_Wgb': 3.359}
    for name, (base, spread) in spreads.items():
        noise = np.random.default_rng([zlib.crc32(name.encode()), seed]).standard_normal(out[name].shape)
        drawn = base * np.exp(spread * noise) if base else spread * noise
        out[name] = jnp.asarray(drawn.astype(out[name].dtype))
    for name, factor in factors.items():
        out[name] = (out[name] * factor).astype(out[name].dtype)
    return out
```

```python
import math
from contextlib import ExitStack

import numpy as np
import concourse.bass as bass
from concourse import mybir

F32 = mybir.dt.float32
BF16 = mybir.dt.bfloat16
U8 = mybir.dt.uint8
ALU = mybir.AluOpType
ACT = mybir.ActivationFunctionType
AX = mybir.AxisListType.X

P = 128
T = 2048
D = 512
NT = T // P
KC = D // P
LN_EPS = 1e-5

H0, D0 = 16, 32
E, F = 8, 352
UNITS = 12
FT = [(0, 128), (128, 128), (256, 96)]
TB = 512
H1, D1 = 16, 128
G = 4
LEVELS = [1, 2, 4, 8, 16, 32, 64]
KDA_EPS = 1e-6
CONV = 4
TH_X, TH_W, SC_W = 0.33, 0.2, 0.6


class Phase(ExitStack):

    def __init__(self):
        super().__init__()
        self.sems = []

    def block(self, nc):
        self.callback(self.clear, nc)
        return self.enter_context(nc.Block())

    def clear(self, nc):
        with nc.Block() as block:
            @block.gpsimd
            def _(pool):
                for sem in self.sems:
                    pool.sem_clear(sem)


class Signal:

    def __init__(self, ctx, nc, name, lead=0):
        self.sem = ctx.enter_context(nc.semaphore(name))
        ctx.sems.append(self.sem)
        self.lead = lead

    def start(self, eng):
        if self.lead:
            eng.sem_inc(self.sem, self.lead)

    def of(self, n):
        return n + (1 + self.lead)


class Chain:

    def __init__(self, ctx, nc, name):
        self.sem = ctx.enter_context(nc.semaphore(name))
        ctx.sems.append(self.sem)
        self.n = 0

    def done(self, ins):
        self.n += 1
        return ins.then_inc(self.sem, 1)

    def settle(self, eng):
        eng.wait_ge(self.sem, self.n)

    def restart(self, eng):
        eng.wait_ge(self.sem, self.n)
        eng.sem_clear(self.sem)
        self.n = 0


LN_EXP_SET = 6


def load_tables(nc, act, number):
    act.add_instruction(mybir.InstLoadActFuncSet(name=nc.get_next_instruction_name(), act_func_set_id=number))


def after(eng, idle, sem, value):
    eng.wait_ge(sem, value)
    eng.sem_inc(idle, 1)


def bc(ap, axis, shape):
    return ap.unsqueeze(axis).to_broadcast(shape)


class Held:
    pass


def phase_modulation(nc, A, K):
    with Phase() as ctx:
        sb = lambda n, s, d=F32: ctx.enter_context(nc.sbuf_tensor("m_" + n, s, d))
        wm = sb("wm", [P, KC, 6 * D])
        c_col = sb("c_col", [P, 2, KC])
        c_act = sb("c_act", [P, 2, KC])
        c_bc = sb("c_bc", [P, KC, P])
        row = sb("row", [1, 4 * D])
        gate = sb("gate", [P, D])
        half = sb("half", [P, D])
        ps = [ctx.enter_context(nc.psum_tensor(f"m_ps{i}", [P, D], F32)) for i in range(6)]
        s_in = Signal(ctx, nc, "m_loaded")
        s_w = Signal(ctx, nc, "m_wmod_loaded")
        s_silu = Signal(ctx, nc, "m_silu")
        s_bc = Signal(ctx, nc, "m_c_spread")
        s_mm = Signal(ctx, nc, "m_products")
        s_row = Signal(ctx, nc, "m_row_copied")
        s_gate = Signal(ctx, nc, "m_gates")
        s_out = Signal(ctx, nc, "m_row_stored")
        s_col = Signal(ctx, nc, "m_columns")
        s_const = Signal(ctx, nc, "m_constants")
        ch = Chain(ctx, nc, "m_dve_chain")
        block = ctx.block(nc)
        wmod = [A["L0_wmod"], A["L1_wmod"]]
        cs = [A["L0_c"], A["L1_c"]]
        COLS = {0: 0, 1: 1, 3: 2, 4: 3}

        @block.sync
        def _(sp):
            for l in range(2):
                sp.dma_start(c_col[:, l, :], cs[l].rearrange("a (k p) -> p (a k)", p=P), allow_slow_non_contiguous=True).then_inc(s_in.sem, 16)
            for l in range(2):
                if l == 1:
                    sp.wait_ge(s_mm.sem, 6)
                sp.dma_start(wm[:, :, :], wmod[l].rearrange("(k p) n -> p k n", p=P)).then_inc(s_w.sem, 16)
                if l == 0:
                    sp.dma_start(K.x[:, :, :], A["L0_attn_x"].rearrange("a (n p) d -> p (a n) d", p=P)).then_inc(s_const.sem, 16)
                    sp.dma_start(K.ident[:, :], A["const_ident"]).then_inc(s_const.sem, 16)
                sp.wait_ge(s_row.sem, 4 * (l + 1))
                sp.dma_start(A["mod_scr"][l:l + 1, :], row[:, :]).then_inc(s_out.sem, 16)
                sp.wait_ge(s_out.sem, 16 * (l + 1))
                sp.dma_start(K.cols[:, l, :, :], A["mod_scr"][l, :].rearrange("(v k p) -> p v k", v=4, p=P), allow_slow_non_contiguous=True).then_inc(s_col.sem, 16)
                sp.wait_ge(s_col.sem, 16 * (l + 1))
            sp.wait_ge(s_const.sem, 32)

        @block.scalar
        def _(act):
            act.wait_ge(s_in.sem, 32)
            act.activation(c_act[:, :, :], c_col[:, :, :], ACT.Silu).then_inc(s_silu.sem, 1)
            for l in range(2):
                for v in range(6):
                    if v in COLS:
                        act.wait_ge(s_mm.sem, 6 * l + v + 1)
                        if l == 1 and COLS[v] == 0:
                            act.wait_ge(s_out.sem, 16)
                        act.activation(row[0:1, COLS[v] * D:(COLS[v] + 1) * D], ps[v][0:1, :], ACT.Copy).then_inc(s_row.sem, 1)

        @block.vector
        def _(v_):
            v_.memset(K.eps[:, 0:1], LN_EPS)
            v_.memset(K.eps[:, 1:2], KDA_EPS)
            v_.memset(K.eps[:, 2:3], math.log(D1 ** -0.5))
            v_.memset(K.zero[:, :], 0.0)
            v_.wait_ge(s_silu.sem, 1)
            for l in range(2):
                if l:
                    v_.wait_ge(s_mm.sem, 6)
                v_.tensor_copy(c_bc[:, :, :], bc(c_act[:, l, :], 2, [P, KC, P])).then_inc(s_bc.sem, 1)
                for g, v in enumerate((2, 5)):
                    v_.wait_ge(s_mm.sem, 6 * l + v + 1)
                    ch.done(v_.tensor_scalar(half[:, :], ps[v][:, :], 0.0, 0.5, ALU.is_ge, ALU.subtract))
                    ch.done(v_.tensor_scalar(gate[:, :], ps[v][:, :], -1.0, 0.25, ALU.mult, ALU.max))
                    ch.settle(v_)
                    ch.done(v_.tensor_tensor(gate[:, :], gate[:, :], ps[v][:, :], ALU.max))
                    ch.settle(v_)
                    ch.done(v_.tensor_scalar(gate[:, :], gate[:, :], 2.0, None, ALU.mult))
                    ch.settle(v_)
                    v_.tensor_tensor(K.gates[:, l, g, :], gate[:, :], half[:, :], ALU.mult).then_inc(s_gate.sem, 1)
                    v_.wait_ge(s_gate.sem, 2 * l + g + 1)
                v_.wait_ge(s_col.sem, 16 * (l + 1))
                for v in (1, 3):
                    v_.tensor_scalar(K.cols[:, l, v, :], K.cols[:, l, v, :], 1.0, None, ALU.add)

        @block.tensor
        def _(pe):
            for l in range(2):
                pe.wait_ge(s_w.sem, 16 * (l + 1))
                pe.wait_ge(s_bc.sem, l + 1)
                for v in range(6):
                    if l:
                        if v in COLS:
                            pe.wait_ge(s_row.sem, COLS[v] + 1)
                        else:
                            pe.wait_ge(s_gate.sem, (2, 5).index(v) + 1)
                    for k in range(KC):
                        last = pe.matmul(ps[v][:, :], c_bc[:, k, :], wm[:, k, v * D:(v + 1) * D], start=(k == 0), stop=(k == KC - 1))
                    last.then_inc(s_mm.sem, 1)


def norm_statistics(dve, ch, stats, mv, x):
    ch.done(dve.bn_stats(stats, x))
    ch.settle(dve)
    return dve.bn_aggr(mv, stats)


def phase_qkv(nc, A, K):
    with Phase() as ctx:
        sb = lambda n, s, d=F32: ctx.enter_context(nc.sbuf_tensor("q_" + n, s, d))
        w = sb("w", [P, KC, 3 * D])
        cs = sb("cs", [P, NT, 2, D0 // 2])
        stats = sb("stats", [P, 2, 6])
        mv = sb("mv", [P, 2, 2])
        rstd = sb("rstd", [P, 2, 2])
        xn = sb("xn", [P, 2, D])
        hT = sb("hT", [P, 2, KC, P])
        raw = sb("raw", [P, 2, 2 * D])
        v = sb("v", [P, 2, D])
        t1 = sb("t1", [P, D])
        t2 = sb("t2", [P, D])
        t3 = sb("t3", [P, D])
        t4 = sb("t4", [P, D])
        rot = sb("rot", [P, 2, 2 * D])
        parts = sb("parts", [P, 3, 8, 2, P], BF16)
        rest = sb("rest", [P, 8, P])
        psx = ctx.enter_context(nc.psum_tensor("q_psx", [P, KC, P], F32))
        psq = ctx.enter_context(nc.psum_tensor("q_psq", [P, 3, D], F32))
        psr = ctx.enter_context(nc.psum_tensor("q_psr", [P, 8, P], F32))
        loaded = Signal(ctx, nc, "q_loaded")
        s_mv = Signal(ctx, nc, "q_mean_var")
        s_rstd = Signal(ctx, nc, "q_rstd", 0)
        s_xn = Signal(ctx, nc, "q_normed", 2)
        s_xT = Signal(ctx, nc, "q_x_turned", 2)
        s_hT = Signal(ctx, nc, "q_h", 1)
        s_qkv = Signal(ctx, nc, "q_products", 2)
        s_raw = Signal(ctx, nc, "q_copied", 1)
        s_rot = Signal(ctx, nc, "q_rotated", 2)
        s_rT = Signal(ctx, nc, "q_heads_turned", 2)
        s_qkT = Signal(ctx, nc, "q_heads_copied", 1)
        s_high = Signal(ctx, nc, "q_high_parts")
        s_rest = Signal(ctx, nc, "q_rests", 1)
        s_mid = Signal(ctx, nc, "q_middle_parts")
        s_st = [Signal(ctx, nc, f"q_v_stored{i}") for i in range(2)]
        s_qst = Signal(ctx, nc, "q_heads_stored")
        cd = Chain(ctx, nc, "q_dve_chain")
        ca = Chain(ctx, nc, "q_act_chain")
        block = ctx.block(nc)
        qk_scr = A["qk_scr"].rearrange("e (g p) t -> p (e g) t", p=P)

        @block.sync
        def _(sp):
            sp.dma_start(w[:, :, :], A["L0_attn_Wqkv"].rearrange("(k p) n -> p k n", p=P)).then_inc(loaded.sem, 16)
            sp.dma_start(cs[:, :, :, :], A["const_rope"].rearrange("(n p) a i -> p n a i", p=P)).then_inc(loaded.sem, 16)
            for b in range(2):
                sp.sem_inc(s_st[b].sem, 16)
            sp.sem_inc(s_qst.sem, 16)
            with sp.Fori(0, NT // 2) as it:
                for b in range(2):
                    n = it * 2 + b
                    after(sp, K.idle, s_raw.sem, s_raw.of(n))
                    sp.dma_start(A["v_scr"][bass.ds(n * P, P), :], v[:, b, :]).then_inc(s_st[b].sem, 16)
                after(sp, K.idle, s_qkT.sem, s_qkT.of(n))
                sp.dma_start(qk_scr[:, :, bass.ds(it * (2 * P), 2 * P)], parts[:, :, :, :, :].rearrange("p e g b n -> p (e g) (b n)")).then_inc(s_qst.sem, 16)
            for b in range(2):
                sp.wait_ge(s_st[b].sem, 16 * (NT // 2) + 16)
            sp.wait_ge(s_qst.sem, 16 * (NT // 2) + 16)

        @block.scalar
        def _(act):
            s_hT.start(act)
            s_raw.start(act)
            load_tables(nc, act, LN_EXP_SET)
            act.wait_ge(loaded.sem, 32)
            with act.Fori(0, NT // 2) as it:
                for b in range(2):
                    n = it * 2 + b
                    act.wait_ge(s_mv.sem, s_mv.of(n))
                    ca.done(act.activation(rstd[:, b, 0:1], mv[:, b, 1:2], ACT.Ln, bias=K.eps[:, 0:1]))
                    ca.settle(act)
                    ca.done(act.activation(rstd[:, b, 1:2], rstd[:, b, 0:1], ACT.Exp, scale=-0.5))
                    ca.settle(act)
                    act.nop().then_inc(s_rstd.sem, 1)
                    act.wait_ge(s_xT.sem, s_xT.of(n))
                    for k in range(KC):
                        ins = act.activation(hT[:, b, k, :], psx[:, k, :], ACT.Identity, bias=K.cols[:, 0, 0, k:k + 1], scale=K.cols[:, 0, 1, k:k + 1])
                    ins.then_inc(s_hT.sem, 1)
                    act.wait_ge(s_qkv.sem, s_qkv.of(n))
                    act.wait_ge(s_rot.sem, s_rot.of(n - 2))
                    act.wait_ge(s_st[b].sem, it * 16 + 16)
                    act.activation(raw[:, b, 0:D], psq[:, 0, :], ACT.Copy)
                    act.activation(raw[:, b, D:2 * D], psq[:, 1, :], ACT.Copy)
                    act.activation(v[:, b, :], psq[:, 2, :], ACT.Copy).then_inc(s_raw.sem, 1)
                    act.wait_ge(s_rT.sem, s_rT.of(n))
                    if b == 0:
                        act.wait_ge(s_qst.sem, it * 16 + 16)
                    act.activation(parts[:, 0, 0:4, b, :], psr[:, 0:4, :], ACT.Copy)
                    act.activation(parts[:, 0, 4:8, b, :], psr[:, 4:8, :], ACT.Copy).then_inc(s_high.sem, 1)
                    act.wait_ge(s_rest.sem, s_rest.of(n))
                    act.activation(parts[:, 1, :, b, :], rest[:, :, :], ACT.Copy).then_inc(s_mid.sem, 1)
                ca.restart(act)

        @block.vector
        def _(dve):
            s_xn.start(dve)
            s_rot.start(dve)
            s_rest.start(dve)
            s_qkT.start(dve)
            dve.wait_ge(loaded.sem, 32)
            with dve.Fori(0, NT // 2) as it:
                for b in range(2):
                    n = it * 2 + b
                    norm_statistics(dve, cd, stats[:, b, :], mv[:, b, :], K.x[:, n, :]).then_inc(s_mv.sem, 1)
                    dve.wait_ge(s_rstd.sem, s_rstd.of(n))
                    dve.wait_ge(s_xT.sem, s_xT.of(n - 2))
                    dve.tensor_scalar(xn[:, b, :], K.x[:, n, :], mv[:, b, 0:1], rstd[:, b, 1:2], ALU.subtract, ALU.mult).then_inc(s_xn.sem, 1)
                    dve.wait_ge(s_raw.sem, s_raw.of(n))
                    dve.wait_ge(s_rT.sem, s_rT.of(n - 2))
                    pairs = raw[:, b, :].rearrange("p (h i e) -> p h i e", h=2 * H0, e=2)
                    turned = rot[:, b, :].rearrange("p (h i e) -> p h i e", h=2 * H0, e=2)
                    four = [t[:, :].rearrange("p (h i) -> p h i", h=2 * H0) for t in (t1, t2, t3, t4)]
                    cos = bc(cs[:, n, 0, :], 1, [P, 2 * H0, D0 // 2])
                    sin = bc(cs[:, n, 1, :], 1, [P, 2 * H0, D0 // 2])
                    cd.done(dve.tensor_tensor(four[0], pairs[:, :, :, 0], cos, ALU.mult))
                    cd.done(dve.tensor_tensor(four[1], pairs[:, :, :, 1], sin, ALU.mult))
                    cd.done(dve.tensor_tensor(four[2], pairs[:, :, :, 0], sin, ALU.mult))
                    cd.done(dve.tensor_tensor(four[3], pairs[:, :, :, 1], cos, ALU.mult))
                    cd.settle(dve)
                    cd.done(dve.tensor_tensor(turned[:, :, :, 0], four[0], four[1], ALU.subtract))
                    cd.done(dve.tensor_tensor(turned[:, :, :, 1], four[2], four[3], ALU.add))
                    cd.settle(dve)
                    dve.nop().then_inc(s_rot.sem, 1)
                    dve.wait_ge(s_high.sem, s_high.of(n))
                    for j in (0, 4):
                        ins = dve.tensor_tensor(rest[:, j:j + 4, :], psr[:, j:j + 4, :], parts[:, 0, j:j + 4, b, :], ALU.subtract)
                    ins.then_inc(s_rest.sem, 1)
                    dve.wait_ge(s_mid.sem, s_mid.of(n))
                    dve.tensor_tensor(parts[:, 2, :, b, :], rest[:, :, :], parts[:, 1, :, b, :], ALU.subtract).then_inc(s_qkT.sem, 1)
                cd.restart(dve)

        @block.tensor
        def _(pe):
            s_xT.start(pe)
            s_qkv.start(pe)
            s_rT.start(pe)
            pe.wait_ge(loaded.sem, 32)
            with pe.Fori(0, NT // 2) as it:
                for b in range(2):
                    n = it * 2 + b
                    pe.wait_ge(s_xn.sem, s_xn.of(n))
                    pe.wait_ge(s_hT.sem, s_hT.of(n - 1))
                    for k in range(KC):
                        ins = pe.transpose(psx[:, k, :], xn[:, b, k * P:(k + 1) * P], K.ident[:, :])
                    ins.then_inc(s_xT.sem, 1)
                    pe.wait_ge(s_hT.sem, s_hT.of(n))
                    pe.wait_ge(s_raw.sem, s_raw.of(n - 1))
                    for j in range(3):
                        for k in range(KC):
                            ins = pe.matmul(psq[:, j, :], hT[:, b, k, :], w[:, k, j * D:(j + 1) * D], start=(k == 0), stop=(k == KC - 1))
                    ins.then_inc(s_qkv.sem, 1)
                    pe.wait_ge(s_rot.sem, s_rot.of(n))
                    pe.wait_ge(s_rest.sem, s_rest.of(n - 1))
                    for j in range(8):
                        ins = pe.transpose(psr[:, j, :], rot[:, b, j * P:(j + 1) * P], K.ident[:, :])
                    ins.then_inc(s_rT.sem, 1)


def phase_attention(nc, A, K, o_all):
    PAIR = 2
    TURNS = H0 // PAIR
    U = PAIR * NT
    banks = lambda q: (q + 4) // 4
    width = lambda q, k: min(D, (q + 1) * P - k * D)
    groups = [(j, q, k, min(4, q + 1 - k)) for j in range(PAIR) for q in range(NT) for k in range(0, q + 1, 4)]
    GT = len(groups)
    assert GT % 2 == 0
    HG = GT // 2
    last_group = {(j, q): max(i for i, g in enumerate(groups) if g[:2] == (j, q)) for j in range(PAIR) for q in range(NT)}
    SC = D0 ** -0.5
    units = [(j, q) for j in range(PAIR) for q in range(NT)]
    SB = sum(banks(q) for _, q in units)
    NBK = 4
    assert SB % NBK == 0
    bank0 = [sum(banks(q) for _, q in units[:n]) for n in range(U + 1)]
    EXP_AT = 0.8
    LAG = 2

    def groups_of(n):
        return [i for i, g in enumerate(groups) if g[:2] == units[n]]

    def spread(main, side, main_at, side_at):
        out = [(main_at + i / max(len(main), 1), 0, v) for i, v in enumerate(main)] + [(side_at(i, len(side)), 1, v) for i, v in enumerate(side)]
        return [(w, v) for _, w, v in sorted(out, key=lambda z: z[:2])]

    with Phase() as ctx:
        sb = lambda n, s, d=F32: ctx.enter_context(nc.sbuf_tensor("a_" + n, s, d))
        QP, KP = ((0, 0, 1, 1), (2, 2, 0, 1)), ((0, 1, 0, 1), (0, 1, 2, 2))
        q_ = sb("q", [P, PAIR, 2, T], BF16)
        k_ = sb("k", [P, PAIR, 2, T], BF16)
        VW = 96
        v_ = sb("v", [P, PAIR, NT, VW])
        mraw = sb("mraw", [P, P])
        mask = sb("mask", [P, P], BF16)
        idb = sb("idb", [P, P], BF16)
        prob = sb("prob", [P, 4, T])
        pT = sb("pT", [P, 2, 4, P])
        mx = sb("mx", [P, 2, 4])
        m = sb("m", [P, 2])
        nb = sb("nb", [P, 2])
        rs = sb("rs", [P, 4, 4])
        rsum = sb("rsum", [P, 2])
        rinv = sb("rinv", [P, 2])
        psS = ctx.enter_context(nc.psum_tensor("a_psS", [P, 4, D], F32))
        psT = [ctx.enter_context(nc.psum_tensor(f"a_psT{i}", [P, 4, P], F32)) for i in range(2)]
        psO = [ctx.enter_context(nc.psum_tensor(f"a_psO{i}", [P, D], F32)) for i in range(2)]
        s_const = Signal(ctx, nc, "a_constants")
        s_in = [Signal(ctx, nc, f"a_head_loaded{i}") for i in range(PAIR)]
        s_zero = Signal(ctx, nc, "a_constants_made")
        s_sc = Signal(ctx, nc, "a_scores")
        s_nb = Signal(ctx, nc, "a_max")
        s_ex = Signal(ctx, nc, "a_exp", 8)
        s_pT = Signal(ctx, nc, "a_probs_turned")
        s_cp = [Signal(ctx, nc, "a_copied_even", 1), Signal(ctx, nc, "a_copied_odd", 1)]
        s_pv = Signal(ctx, nc, "a_values", GT)
        s_o = Signal(ctx, nc, "a_out", 4)
        cd = Chain(ctx, nc, "a_dve_chain")
        block = ctx.block(nc)

        @block.sync
        def _(sp):
            sp.dma_start(mraw[:, :], A["const_causal"]).then_inc(s_const.sem, 16)
            with sp.Fori(0, TURNS) as it:
                for j in range(PAIR):
                    h = it * PAIR + j
                    after(sp, K.idle, s_pv.sem, s_pv.of(it * GT + (last_group[j, NT - 1] - GT)))
                    for to, parts, at in ((q_, QP, 0), (k_, KP, D)):
                        for r in range(2):
                            for i, part in enumerate(parts[r]):
                                sp.dma_start(to[i * D0:(i + 1) * D0, j, r, :], A["qk_scr"][part, bass.ds(h * D0 + at, D0), :]).then_inc(s_in[j].sem, 16)
                    sp.dma_start(v_[:, j, :, 0:D0], A["v_scr"].rearrange("(n p) c -> p n c", p=P)[:, :, bass.ds(h * D0, D0)]).then_inc(s_in[j].sem, 16)

        @block.tensor
        def _(pe):
            s_pT.start(pe)
            s_pv.start(pe)
            pe.wait_ge(s_zero.sem, 1)

            def scores(it, n, k):
                j, q = units[n]
                i = bank0[n] + k
                w = width(q, k)
                last = k == banks(q) - 1
                pe.wait_ge(s_ex.sem, s_ex.of(it * SB + (i - NBK)))
                for r in range(2):
                    ins = pe.matmul(psS[:, i % NBK, 0:w], q_[:, j, r, q * P:(q + 1) * P], k_[:, j, r, k * D:k * D + w], start=(r == 0), stop=(r == 1 and not last))
                if last:
                    ins = pe.matmul(psS[:, i % NBK, w - P:w], mask[:, :], idb[:, :], start=False, stop=True)
                ins.then_inc(s_sc.sem, 1)

            def turn(it, g):
                j, q, k, n = groups[g]
                u = j * NT + q
                pe.wait_ge(s_cp[g % 2].sem, s_cp[g % 2].of(it * HG + (g // 2 - 1)))
                pe.wait_ge(s_ex.sem, s_ex.of(it * SB + (bank0[u] + k // 4)))
                for i in range(n):
                    ins = pe.transpose(psT[g % 2][:, i, :], prob[:, u % 4, (k + i) * P:(k + i + 1) * P], K.ident[:, :])
                ins.then_inc(s_pT.sem, 1)

            def values(it, g):
                j, q, k, n = groups[g]
                u = it * U + j * NT + q
                pe.wait_ge(s_cp[g % 2].sem, s_cp[g % 2].of(it * HG + g // 2))
                if k == 0:
                    pe.wait_ge(s_o.sem, s_o.of(u - 2))
                for i in range(n):
                    ins = pe.matmul(psO[q % 2][:, 0:VW], pT[:, g % 2, i, :], v_[:, j, k + i, :], start=(k + i == 0), stop=(k + i == q))
                ins.then_inc(s_pv.sem, 1)

            with pe.Fori(0, TURNS) as it:
                for n in range(U + LAG):
                    if n < U and units[n][1] == 0:
                        j = units[n][0]
                        pe.wait_ge(s_in[j].sem, it * 272 + 272)
                    now = range(banks(units[n][1])) if n < U else []
                    old = groups_of(n - LAG) if n >= LAG else []
                    for which, v in spread(now, old, 0, lambda i, m: (i + 1) / (m + 1)):
                        if which == 0:
                            scores(it, n, v)
                        else:
                            turn(it, v)
                            if v:
                                values(it, v - 1)
                values(it, GT - 1)

        @block.scalar
        def _(act):
            s_ex.start(act)
            s_cp[1].start(act)

            def copy(it, g):
                act.wait_ge(s_pT.sem, s_pT.of(it * GT + g))
                act.wait_ge(s_pv.sem, s_pv.of(it * GT + (g - 2)))
                n = groups[g][3]
                act.activation(pT[:, 1, 0:n, :], psT[1][:, 0:n, :], ACT.Copy).then_inc(s_cp[1].sem, 1)

            def exponentials(it, n, k):
                j, q = units[n]
                if k == 0:
                    act.wait_ge(s_nb.sem, s_nb.of(it * U + n))
                    act.wait_ge(s_o.sem, s_o.of(it * U + (n - 4)))
                w = width(q, k)
                act.activation(prob[:, n % 4, k * D:k * D + w], psS[:, (bank0[n] + k) % NBK, 0:w], ACT.Exp, bias=nb[:, q % 2:q % 2 + 1], scale=SC,
                               accum_out=rs[:, q % 4, k:k + 1]).then_inc(s_ex.sem, 1)

            with act.Fori(0, TURNS) as it:
                for n in range(U + LAG):
                    now = range(banks(units[n][1])) if n < U else []
                    old = groups_of(n - LAG) if n >= LAG else []
                    for which, v in spread(now, old, EXP_AT, lambda i, m: (i + 1) / (m + 1)):
                        if which == 0:
                            exponentials(it, n, v)
                        elif v % 2:
                            copy(it, v)

        @block.vector
        def _(dve):
            s_cp[0].start(dve)
            s_o.start(dve)
            dve.tensor_copy(idb[:, :], K.ident[:, :])
            dve.wait_ge(s_const.sem, 16)
            dve.tensor_copy(mask[:, :], mraw[:, :])
            dve.memset(v_[:, :, :, D0:], 0.0).then_inc(s_zero.sem, 1)

            def copy(it, g):
                dve.wait_ge(s_pT.sem, s_pT.of(it * GT + g))
                dve.wait_ge(s_pv.sem, s_pv.of(it * GT + (g - 2)))
                n = groups[g][3]
                dve.tensor_copy(pT[:, 0, 0:n, :], psT[0][:, 0:n, :]).then_inc(s_cp[0].sem, 1)

            def maximum(it, n, k):
                j, q = units[n]
                b = q % 2
                i = bank0[n] + k
                dve.wait_ge(s_sc.sem, s_sc.of(it * SB + i))
                if banks(q) == 1:
                    cd.done(dve.tensor_reduce(m[:, b:b + 1], psS[:, i % NBK, 0:width(q, k)], AX, ALU.max))
                else:
                    cd.done(dve.tensor_reduce(mx[:, b, k:k + 1], psS[:, i % NBK, 0:width(q, k)], AX, ALU.max))
                if k < banks(q) - 1:
                    return
                cd.settle(dve)
                if k:
                    cd.done(dve.tensor_reduce(m[:, b:b + 1], mx[:, b, 0:banks(q)], AX, ALU.max))
                    cd.settle(dve)
                back = bank0[n - 1] - 1 if n >= 2 else bank0[n - 1 + U] - 1 - SB if n == 0 else -1
                dve.wait_ge(s_ex.sem, s_ex.of(it * SB + back))
                dve.tensor_scalar(nb[:, b:b + 1], m[:, b:b + 1], -SC, None, ALU.mult).then_inc(s_nb.sem, 1)

            def finish(it, n):
                j, q = units[n]
                u = it * U + n
                b = q % 2
                dve.wait_ge(s_ex.sem, s_ex.of(it * SB + (bank0[n + 1] - 1)))
                cd.done(dve.tensor_reduce(rsum[:, b:b + 1], rs[:, q % 4, 0:banks(q)], AX, ALU.add))
                cd.settle(dve)
                cd.done(dve.reciprocal(rinv[:, b:b + 1], rsum[:, b:b + 1]))
                cd.settle(dve)
                dve.wait_ge(s_pv.sem, s_pv.of(it * GT + last_group[j, q]))
                dve.tensor_scalar(o_all[:, q, bass.ds((it * PAIR + j) * D0, D0)], psO[b][:, 0:D0], rinv[:, b:b + 1], None, ALU.mult).then_inc(s_o.sem, 1)

            with dve.Fori(0, TURNS) as it:
                for n in range(U + LAG):
                    now = range(banks(units[n][1])) if n < U else []
                    old = groups_of(n - LAG) if n >= LAG else []
                    for which, v in spread(now, old, 0, lambda i, m: (i + 1) / (m + 1) + 0.05):
                        if which == 0:
                            maximum(it, n, v)
                        elif v % 2 == 0:
                            copy(it, v)
                    if n >= LAG + 1:
                        finish(it, n - LAG - 1)
                finish(it, U - 1)
                cd.restart(dve)



def phase_attention_out(nc, A, K, o_all):
    with Phase() as ctx:
        sb = lambda n, s, d=F32: ctx.enter_context(nc.sbuf_tensor("r_" + n, s, d))
        wo = sb("wo", [P, KC, D])
        wr = sb("wr", [P, KC, E + 1])
        tri = sb("tri", [P, E, E])
        o = sb("o", [P, 2, D])
        oT = sb("oT", [P, 2, KC, P])
        y = sb("y", [P, 2, D])
        stats = sb("stats", [P, 2, 6])
        mv = sb("mv", [P, 2, 2])
        rstd = sb("rstd", [P, 2, 2])
        xn = sb("xn", [P, 2, D])
        hT = sb("hT", [P, 2, KC, P])
        nm = sb("nm", [P, 2])
        ex = sb("ex", [P, 2, E + 1])
        den = sb("den", [P, 2, 2])
        inv = sb("inv", [P, 2, 2])
        prob = sb("prob", [P, 2, E])
        gt = sb("gt", [P, 2, E, E])
        eq = sb("eq", [P, 2, E, E])
        rank = sb("rank", [P, 2, E])
        cw = sb("cw", [P, 2, UNITS])
        cT = sb("cT", [UNITS, 2, P])
        ps = lambda n, s: ctx.enter_context(nc.psum_tensor("r_" + n, s, F32))
        ps_oT, ps_y, ps_xT, ps_l, ps_c = ps("ps_oT", [P, KC, P]), ps("ps_y", [P, D]), ps("ps_xT", [P, KC, P]), ps("ps_l", [P, D]), ps("ps_c", [P, D])
        S = lambda n, lead=0: Signal(ctx, nc, "r_" + n, lead)
        loaded = S("loaded")
        s_o = S("o_copied")
        s_oT, s_oTc = S("o_turned", 2), S("o_turned_copied", 1)
        s_y, s_x = S("product", 1), S("x_summed", 1)
        s_mv, s_rstd, s_xn, s_xT, s_hT, s_hc = S("mean_var"), S("rstd"), S("normed"), S("x_turned", 2), S("h", 1), S("h_kept", 2)
        s_l, s_nm, s_ex, s_cw, s_c, s_cT = S("logits", 2), S("max"), S("exp", 1), S("weights"), S("weights_turned", 2), S("weights_copied", 1)
        s_st = [Signal(ctx, nc, f"r_stored{i}", 0) for i in range(2)]
        cd, ca = Chain(ctx, nc, "r_dve_chain"), Chain(ctx, nc, "r_act_chain")
        block = ctx.block(nc)

        @block.sync
        def _(sp):
            sp.dma_start(wo[:, :, :], A["L0_attn_Wo"].rearrange("(k p) n -> p k n", p=P)).then_inc(loaded.sem, 16)
            with nc.allow_non_contiguous_dma(reason="router weights, a few KB"):
                sp.dma_start(wr[:, :, 0:E], A["L0_ffn_Wr"].rearrange("(k p) n -> p k n", p=P)).then_inc(loaded.sem, 16)
                sp.dma_start(wr[:, :, E:E + 1], A["L0_ffn_Wsg"].rearrange("(k p) n -> p k n", p=P)).then_inc(loaded.sem, 16)
            sp.dma_start(tri[:, :, :], A["const_before"].partition_broadcast(P)).then_inc(loaded.sem, 16)
            for b in range(2):
                sp.sem_inc(s_st[b].sem, 16)
            with sp.Fori(0, NT // 2) as it:
                for b in range(2):
                    n = it * 2 + b
                    after(sp, K.idle, s_cT.sem, s_cT.of(n))
                    sp.dma_start(A["ct_scr"][:, bass.ds(n * P, P)], cT[:, b, :]).then_inc(s_st[b].sem, 16)
            for b in range(2):
                sp.wait_ge(s_st[b].sem, 16 * (NT // 2) + 16)

        @block.gpsimd
        def _(pool):
            s_hc.start(pool)
            with pool.Fori(0, NT // 2) as it:
                for b in range(2):
                    n = it * 2 + b
                    after(pool, K.idle, s_oT.sem, s_oT.of(n - 2))
                    pool.tensor_copy(o[:, b, :], o_all[:, n, :]).then_inc(s_o.sem, 1)
                    after(pool, K.idle, s_hT.sem, s_hT.of(n))
                    pool.tensor_copy(K.hT[:, :, bass.ds(n * P, P)], hT[:, b, :, :]).then_inc(s_hc.sem, 1)

        @block.tensor
        def _(pe):
            for s in (s_oT, s_y, s_xT, s_l, s_c):
                s.start(pe)
            pe.wait_ge(loaded.sem, 64)
            with pe.Fori(0, NT // 2) as it:
                for b in range(2):
                    n = it * 2 + b
                    pe.wait_ge(s_o.sem, s_o.of(n))
                    pe.wait_ge(s_oTc.sem, s_oTc.of(n - 1))
                    for k in range(KC):
                        ins = pe.transpose(ps_oT[:, k, :], o[:, b, k * P:(k + 1) * P], K.ident[:, :])
                    ins.then_inc(s_oT.sem, 1)
                    pe.wait_ge(s_oTc.sem, s_oTc.of(n))
                    pe.wait_ge(s_x.sem, s_x.of(n - 1))
                    for k in range(KC):
                        ins = pe.matmul(ps_y[:, :], oT[:, b, k, :], wo[:, k, :], start=(k == 0), stop=(k == KC - 1))
                    ins.then_inc(s_y.sem, 1)
                    pe.wait_ge(s_xn.sem, s_xn.of(n))
                    pe.wait_ge(s_hT.sem, s_hT.of(n - 1))
                    for k in range(KC):
                        ins = pe.transpose(ps_xT[:, k, :], xn[:, b, k * P:(k + 1) * P], K.ident[:, :])
                    ins.then_inc(s_xT.sem, 1)
                    pe.wait_ge(s_hT.sem, s_hT.of(n))
                    pe.wait_ge(s_ex.sem, s_ex.of(n - 1))
                    for k in range(KC):
                        ins = pe.matmul(ps_l[:, 0:E + 1], hT[:, b, k, :], wr[:, k, :], start=(k == 0), stop=(k == KC - 1))
                    ins.then_inc(s_l.sem, 1)
                    pe.wait_ge(s_cw.sem, s_cw.of(n))
                    pe.wait_ge(s_cT.sem, s_cT.of(n - 1))
                    pe.transpose(ps_c[0:UNITS, 0:P], cw[:, b, :], K.ident[:, :]).then_inc(s_c.sem, 1)

        @block.scalar
        def _(act):
            for s in (s_oTc, s_hT, s_ex, s_cT):
                s.start(act)
            load_tables(nc, act, LN_EXP_SET)
            with act.Fori(0, NT // 2) as it:
                for b in range(2):
                    n = it * 2 + b
                    act.wait_ge(s_oT.sem, s_oT.of(n))
                    act.wait_ge(s_y.sem, s_y.of(n - 1))
                    act.activation(oT[:, b, :, :], ps_oT[:, :, :], ACT.Copy).then_inc(s_oTc.sem, 1)
                    act.wait_ge(s_mv.sem, s_mv.of(n))
                    ca.done(act.activation(rstd[:, b, 0:1], mv[:, b, 1:2], ACT.Ln, bias=K.eps[:, 0:1]))
                    ca.settle(act)
                    act.activation(rstd[:, b, 1:2], rstd[:, b, 0:1], ACT.Exp, scale=-0.5).then_inc(s_rstd.sem, 1)
                    act.wait_ge(s_xT.sem, s_xT.of(n))
                    act.wait_ge(s_hc.sem, s_hc.of(n - 2))
                    for k in range(KC):
                        ins = act.activation(hT[:, b, k, :], ps_xT[:, k, :], ACT.Identity, bias=K.cols[:, 0, 2, k:k + 1], scale=K.cols[:, 0, 3, k:k + 1])
                    ins.then_inc(s_hT.sem, 1)
                    act.wait_ge(s_nm.sem, s_nm.of(n))
                    act.activation(ex[:, b, E:E + 1], ps_l[:, E:E + 1], ACT.Exp, scale=-1.0)
                    act.activation(ex[:, b, 0:E], ps_l[:, 0:E], ACT.Exp, bias=nm[:, b:b + 1], accum_out=den[:, b, 0:1]).then_inc(s_ex.sem, 1)
                    act.wait_ge(s_c.sem, s_c.of(n))
                    act.wait_ge(s_st[b].sem, it * 16 + 16)
                    act.activation(cT[:, b, :], ps_c[0:UNITS, 0:P], ACT.Copy).then_inc(s_cT.sem, 1)
                ca.restart(act)

        @block.vector
        def _(dve):
            s_x.start(dve)
            with dve.Fori(0, NT // 2) as it:
                for b in range(2):
                    n = it * 2 + b
                    dve.wait_ge(s_y.sem, s_y.of(n))
                    cd.done(dve.tensor_tensor(y[:, b, :], ps_y[:, :], K.gates[:, 0, 0, :], ALU.mult))
                    cd.settle(dve)
                    dve.tensor_tensor(K.x[:, n, :], K.x[:, n, :], y[:, b, :], ALU.add).then_inc(s_x.sem, 1)
                    after(dve, K.idle, s_x.sem, s_x.of(n))
                    norm_statistics(dve, cd, stats[:, b, :], mv[:, b, :], K.x[:, n, :]).then_inc(s_mv.sem, 1)
                    dve.wait_ge(s_rstd.sem, s_rstd.of(n))
                    dve.tensor_scalar(xn[:, b, :], K.x[:, n, :], mv[:, b, 0:1], rstd[:, b, 1:2], ALU.subtract, ALU.mult).then_inc(s_xn.sem, 1)
                    dve.wait_ge(s_l.sem, s_l.of(n))
                    dve.tensor_reduce(nm[:, b:b + 1], ps_l[:, 0:E], AX, ALU.max, negate=True).then_inc(s_nm.sem, 1)
                    dve.wait_ge(s_ex.sem, s_ex.of(n))
                    cd.done(dve.tensor_scalar(den[:, b, 1:2], ex[:, b, E:E + 1], 1.0, None, ALU.add))
                    cd.settle(dve)
                    cd.done(dve.reciprocal(inv[:, b, :], den[:, b, :]))
                    cd.settle(dve)
                    cd.done(dve.tensor_scalar(prob[:, b, :], ex[:, b, 0:E], inv[:, b, 0:1], None, ALU.mult))
                    cd.settle(dve)
                    own = bc(prob[:, b, :], 2, [P, E, E])
                    other = bc(prob[:, b, :], 1, [P, E, E])
                    cd.done(dve.tensor_tensor(gt[:, b, :, :], other, own, ALU.is_gt))
                    cd.done(dve.tensor_tensor(eq[:, b, :, :], other, own, ALU.is_equal))
                    cd.settle(dve)
                    cd.done(dve.tensor_tensor(eq[:, b, :, :], eq[:, b, :, :], tri[:, :, :], ALU.mult))
                    cd.settle(dve)
                    cd.done(dve.tensor_tensor(gt[:, b, :, :], gt[:, b, :, :], eq[:, b, :, :], ALU.add))
                    cd.settle(dve)
                    cd.done(dve.tensor_reduce(rank[:, b, :], gt[:, b, :, :], AX, ALU.add))
                    cd.settle(dve)
                    cd.done(dve.tensor_scalar(rank[:, b, :], rank[:, b, :], 2.0, None, ALU.is_lt))
                    cd.settle(dve)
                    cd.done(dve.tensor_tensor(cw[:, b, 0:E], rank[:, b, :], prob[:, b, :], ALU.mult))
                    dve.tensor_copy(cw[:, b, E:UNITS], inv[:, b, 1:2].to_broadcast([P, UNITS - E])).then_inc(s_cw.sem, 1)
                cd.restart(dve)


def phase_mixture(nc, A, K):
    TBN = T // TB
    TPB = TB // P
    NF = len(FT)
    with Phase() as ctx:
        sb = lambda n, s, d=F32: ctx.enter_context(nc.sbuf_tensor("x_" + n, s, d))
        wg = sb("wg", [P, 2, KC, F])
        wu = sb("wu", [P, 2, KC, F])
        wd = sb("wd", [P, 2, NF, D])
        cb = sb("cb", [P, 2, TB])
        sg = sb("sg", [P, 2, TB])
        sc = sb("sc", [P, 2, TB])
        at = sb("at", [P, 2, NF, TB])
        y = sb("y", [P, 2, D])
        psG = [ctx.enter_context(nc.psum_tensor(f"x_psG{i}", [P, TB], F32)) for i in range(2)]
        psU = [ctx.enter_context(nc.psum_tensor(f"x_psU{i}", [P, TB], F32)) for i in range(2)]
        psY = [ctx.enter_context(nc.psum_tensor(f"x_psY{i}", [P, D], F32)) for i in range(TPB)]
        S = lambda n, lead=0: Signal(ctx, nc, "x_" + n, lead)
        s_w = [S(f"weights_loaded{i}") for i in range(2)]
        s_g = S("gate_product", 0)
        s_u = S("up_product", 2)
        s_sg = S("silu", 2)
        s_sc = S("weighted", 2)
        s_at = S("activated", 2 * NF)
        s_y = S("down_product", 2)
        s_x = S("x_summed", TPB)
        cd = Chain(ctx, nc, "x_dve_chain")
        block = ctx.block(nc)
        WB = 5 * 16

        @block.sync
        def _(sp):
            with sp.Fori(0, TBN) as tb:
                with sp.Fori(0, UNITS // 2) as u2:
                    for b in range(2):
                        u = u2 * 2 + b
                        n = tb * UNITS + u2 * 2 + b
                        after(sp, K.idle, s_y.sem, s_y.of(n - 2))
                        sem = s_w[b].sem
                        sp.dma_start(wg[:, b, :, :], A["Wg_all"][bass.ds(u, 1), :, :].rearrange("a (k p) f -> p (a k) f", p=P)).then_inc(sem, 16)
                        sp.dma_start(wu[:, b, :, :], A["Wu_all"][bass.ds(u, 1), :, :].rearrange("a (k p) f -> p (a k) f", p=P)).then_inc(sem, 16)
                        sp.dma_start(wd[:, b, 0:2, :], A["Wd_all"][bass.ds(u, 1), 0:2 * P, :].rearrange("a (k p) f -> p (a k) f", p=P)).then_inc(sem, 16)
                        sp.dma_start(wd[0:F - 2 * P, b, 2, :], A["Wd_all"][bass.ds(u, 1), 2 * P:F, :].rearrange("a p f -> p (a f)")).then_inc(sem, 16)
                        sp.dma_start(cb[:, b, :], A["ct_scr"][bass.ds(u, 1), bass.ds(tb * TB, TB)].rearrange("a t -> (a t)").partition_broadcast(P)).then_inc(sem, 16)

        @block.tensor
        def _(pe):
            s_u.start(pe)
            s_y.start(pe)
            with pe.Fori(0, TBN) as tb:
                with pe.Fori(0, UNITS // 2) as u2:
                    for b in range(2):
                        n = tb * UNITS + u2 * 2 + b
                        pe.wait_ge(s_w[b].sem, tb * (WB * UNITS // 2) + u2 * WB + WB)
                        for f, (f0, fw) in enumerate(FT):
                            i = b * NF + f
                            m = tb * (UNITS * NF) + u2 * (2 * NF) + i
                            pe.wait_ge(s_sg.sem, s_sg.of(m - 2))
                            for k in range(KC):
                                ins = pe.matmul(psG[i % 2][0:fw, :], wg[:, b, k, f0:f0 + fw], K.hT[:, k, bass.ds(tb * TB, TB)], start=(k == 0), stop=(k == KC - 1))
                            ins.then_inc(s_g.sem, 1)
                            pe.wait_ge(s_at.sem, s_at.of(m - 2))
                            for k in range(KC):
                                ins = pe.matmul(psU[i % 2][0:fw, :], wu[:, b, k, f0:f0 + fw], K.hT[:, k, bass.ds(tb * TB, TB)], start=(k == 0), stop=(k == KC - 1))
                            ins.then_inc(s_u.sem, 1)
                        for f, (f0, fw) in enumerate(FT):
                            m = tb * (UNITS * NF) + u2 * (2 * NF) + (b * NF + f)
                            pe.wait_ge(s_at.sem, s_at.of(m))
                            for t in range(TPB):
                                if f == 0:
                                    pe.wait_ge(s_x.sem, s_x.of((n - 1) * TPB + t))
                                ins = pe.matmul(psY[t][:, :], at[0:fw, b, f, t * P:(t + 1) * P], wd[0:fw, b, f, :], start=(f == 0), stop=(f == NF - 1))
                        ins.then_inc(s_y.sem, 1)

        @block.scalar
        def _(act):
            s_sg.start(act)
            with act.Fori(0, TBN) as tb:
                with act.Fori(0, UNITS // 2) as u2:
                    for i in range(2 * NF):
                        fw = FT[i % NF][1]
                        m = tb * (UNITS * NF) + u2 * (2 * NF) + i
                        act.wait_ge(s_g.sem, s_g.of(m))
                        act.wait_ge(s_sc.sem, s_sc.of(m - 2))
                        act.activation(sg[0:fw, i % 2, :], psG[i % 2][0:fw, :], ACT.Silu).then_inc(s_sg.sem, 1)

        @block.gpsimd
        def _(pool):
            s_sc.start(pool)
            with pool.Fori(0, TBN) as tb:
                with pool.Fori(0, UNITS // 2) as u2:
                    for b in range(2):
                        after(pool, K.idle, s_w[b].sem, tb * (WB * UNITS // 2) + u2 * WB + WB)
                        for f, (f0, fw) in enumerate(FT):
                            i = b * NF + f
                            m = tb * (UNITS * NF) + u2 * (2 * NF) + i
                            pool.wait_ge(s_sg.sem, s_sg.of(m))
                            after(pool, K.idle, s_at.sem, s_at.of(m - 2))
                            pool.tensor_tensor(sc[0:fw, i % 2, :], sg[0:fw, i % 2, :], cb[0:fw, b, :], ALU.mult).then_inc(s_sc.sem, 1)

        @block.vector
        def _(dve):
            s_at.start(dve)
            s_x.start(dve)
            with dve.Fori(0, TBN) as tb:
                with dve.Fori(0, UNITS // 2) as u2:
                    for b in range(2):
                        n = tb * UNITS + u2 * 2 + b
                        dve.wait_ge(s_y.sem, s_y.of(n - 2))
                        for f, (f0, fw) in enumerate(FT):
                            i = b * NF + f
                            m = tb * (UNITS * NF) + u2 * (2 * NF) + i
                            dve.wait_ge(s_u.sem, s_u.of(m))
                            dve.wait_ge(s_sc.sem, s_sc.of(m))
                            dve.tensor_tensor(at[0:fw, b, f, :], psU[i % 2][0:fw, :], sc[0:fw, i % 2, :], ALU.mult).then_inc(s_at.sem, 1)
                        dve.wait_ge(s_y.sem, s_y.of(n))
                        for t in range(TPB):
                            cd.done(dve.tensor_tensor(y[:, t % 2, :], psY[t][:, :], K.gates[:, 0, 1, :], ALU.mult))
                            cd.settle(dve)
                            row = K.x[:, tb * TPB + t, :]
                            dve.tensor_tensor(row, row, y[:, t % 2, :], ALU.add).then_inc(s_x.sem, 1)
                    cd.restart(dve)


def phase_kda_inputs(nc, A, K):
    with Phase() as ctx:
        sb = lambda n, s, d=F32: ctx.enter_context(nc.sbuf_tensor("h_" + n, s, d))
        wb = sb("wb", [P, KC, H1])
        stats = sb("stats", [P, 2, 6])
        mv = sb("mv", [P, 2, 2])
        rstd = sb("rstd", [P, 2, 2])
        xn = sb("xn", [P, 2, D])
        hT = sb("hT", [P, 2, KC + 2, P])
        wab = sb("wab", [P, 2, KC, P])
        ez = sb("ez", [P, 2, H1])
        ps_xT = ctx.enter_context(nc.psum_tensor("h_ps_xT", [P, KC, P], F32))
        ps_b = ctx.enter_context(nc.psum_tensor("h_ps_b", [P, D], F32))
        ps_f = ctx.enter_context(nc.psum_tensor("h_ps_f", [P, 2, P], F32))
        S = lambda n, lead=0: Signal(ctx, nc, "h_" + n, lead)
        s_fg, s_fgc = S("low_rank", 1), S("low_rank_copied", 1)
        s_st = [S(f"stored{i}") for i in range(2)]
        loaded = S("loaded")
        s_mv, s_rstd, s_xn, s_xT, s_hT = S("mean_var"), S("rstd"), S("normed"), S("x_turned", 2), S("h", 1)
        s_z, s_ez, s_b = S("beta_product", 2), S("beta_exp", 1), S("beta", 2)
        cd, ca = Chain(ctx, nc, "h_dve_chain"), Chain(ctx, nc, "h_act_chain")
        block = ctx.block(nc)

        @block.sync
        def _(sp):
            with nc.allow_non_contiguous_dma(reason="beta's weights, 32 KB"):
                sp.dma_start(wb[:, :, :], A["L1_attn_Wb"].rearrange("(k p) n -> p k n", p=P)).then_inc(loaded.sem, 16)
            for i, w in enumerate((A["L1_attn_Wfa"], A["L1_attn_Wga"])):
                sp.dma_start(wab[:, i, :, :], w.rearrange("(k p) n -> p k n", p=P)).then_inc(loaded.sem, 16)
            for b in range(2):
                sp.sem_inc(s_st[b].sem, 16)
            with sp.Fori(0, NT // 2) as it:
                for b in range(2):
                    n = it * 2 + b
                    after(sp, K.idle, s_fgc.sem, s_fgc.of(n))
                    sp.dma_start(A["h_scr"][bass.ds(n, 1), :, :].rearrange("a p n -> p (a n)"), hT[:, b, :, :].rearrange("p k n -> p (k n)")).then_inc(s_st[b].sem, 16)
            for b in range(2):
                sp.wait_ge(s_st[b].sem, 16 * (NT // 2) + 16)

        @block.tensor
        def _(pe):
            s_xT.start(pe)
            s_z.start(pe)
            s_fg.start(pe)
            pe.wait_ge(loaded.sem, 48)
            with pe.Fori(0, NT // 2) as it:
                for b in range(2):
                    n = it * 2 + b
                    pe.wait_ge(s_xn.sem, s_xn.of(n))
                    pe.wait_ge(s_hT.sem, s_hT.of(n - 1))
                    for k in range(KC):
                        ins = pe.transpose(ps_xT[:, k, :], xn[:, b, k * P:(k + 1) * P], K.ident[:, :])
                    ins.then_inc(s_xT.sem, 1)
                    pe.wait_ge(s_hT.sem, s_hT.of(n))
                    pe.wait_ge(s_ez.sem, s_ez.of(n - 1))
                    for k in range(KC):
                        ins = pe.matmul(ps_b[:, 0:H1], hT[:, b, k, :], wb[:, k, :], start=(k == 0), stop=(k == KC - 1))
                    ins.then_inc(s_z.sem, 1)
                    pe.wait_ge(s_fgc.sem, s_fgc.of(n - 1))
                    for i in range(2):
                        for k in range(KC):
                            ins = pe.matmul(ps_f[:, i, :], wab[:, i, k, :], hT[:, b, k, :], start=(k == 0), stop=(k == KC - 1))
                    ins.then_inc(s_fg.sem, 1)

        @block.scalar
        def _(act):
            s_hT.start(act)
            s_ez.start(act)
            s_fgc.start(act)
            load_tables(nc, act, LN_EXP_SET)
            with act.Fori(0, NT // 2) as it:
                for b in range(2):
                    n = it * 2 + b
                    act.wait_ge(s_mv.sem, s_mv.of(n))
                    ca.done(act.activation(rstd[:, b, 0:1], mv[:, b, 1:2], ACT.Ln, bias=K.eps[:, 0:1]))
                    ca.settle(act)
                    act.activation(rstd[:, b, 1:2], rstd[:, b, 0:1], ACT.Exp, scale=-0.5).then_inc(s_rstd.sem, 1)
                    act.wait_ge(s_xT.sem, s_xT.of(n))
                    act.wait_ge(s_st[b].sem, it * 16 + 16)
                    for k in range(KC):
                        ins = act.activation(hT[:, b, k, :], ps_xT[:, k, :], ACT.Identity, bias=K.cols[:, 1, 0, k:k + 1], scale=K.cols[:, 1, 1, k:k + 1])
                    ins.then_inc(s_hT.sem, 1)
                    act.wait_ge(s_z.sem, s_z.of(n))
                    act.wait_ge(s_b.sem, s_b.of(n - 2))
                    act.activation(ez[:, b, :], ps_b[:, 0:H1], ACT.Exp, scale=-1.0).then_inc(s_ez.sem, 1)
                    act.wait_ge(s_fg.sem, s_fg.of(n))
                    act.activation(hT[:, b, KC:, :], ps_f[:, :, :], ACT.Copy).then_inc(s_fgc.sem, 1)
                ca.restart(act)

        @block.vector
        def _(dve):
            s_b.start(dve)
            with dve.Fori(0, NT // 2) as it:
                for b in range(2):
                    n = it * 2 + b
                    norm_statistics(dve, cd, stats[:, b, :], mv[:, b, :], K.x[:, n, :]).then_inc(s_mv.sem, 1)
                    dve.wait_ge(s_rstd.sem, s_rstd.of(n))
                    dve.wait_ge(s_xT.sem, s_xT.of(n - 2))
                    dve.tensor_scalar(xn[:, b, :], K.x[:, n, :], mv[:, b, 0:1], rstd[:, b, 1:2], ALU.subtract, ALU.mult).then_inc(s_xn.sem, 1)
                    dve.wait_ge(s_ez.sem, s_ez.of(n))
                    cd.done(dve.tensor_scalar(ez[:, b, :], ez[:, b, :], 1.0, None, ALU.add))
                    cd.settle(dve)
                    dve.reciprocal(K.beta[:, n, :], ez[:, b, :]).then_inc(s_b.sem, 1)
                cd.restart(dve)


def phase_kda(nc, A, K):
    C = NT
    NQ = H1 // G
    NL = len(LEVELS)
    HD = H1 * D1
    with Phase() as ctx:
        sb = lambda n, s, d=F32: ctx.enter_context(nc.sbuf_tensor("d_" + n, s, d))
        w3 = sb("w3", [P, 3, KC, G * D1])
        wfg = sb("wfg", [P, 2, G * D1])
        wo = sb("wo", [P, G, D])
        cw = sb("cw", [P, 3, G, CONV])
        hc = sb("hc", [P, 2, KC + 2, P])
        dtb = sb("dtb", [P, H1])
        nA = sb("nA", [P, H1])
        onw = sb("onw", [P, 1])
        ones = sb("ones", [P, P])
        mean = sb("mean", [P, P])
        mT = sb("mT", [P, NL, P // 2], U8)
        mY = sb("mY", [P, NL - 1, P])
        m1 = sb("m1", [P, P])
        pre = sb("pre", [P, 2, 3, G, CONV - 1 + P])
        acc = sb("acc", [P, 3, G, P])
        qkv = sb("qkv", [P, 3, G, P])
        sq = sb("sq", [P, G, P])
        rn = sb("rn", [P, G, P])
        xg = sb("xg", [P, G, P])
        mraw = xg[:, :, :].rearrange("p g n -> p (g n)")[:, 0:NL * (P // 2)]
        e1 = sb("e1", [P, G, P])
        e2 = sb("e2", [P, G, P])
        e3 = sb("e3", [P, G, P])
        em = sb("em", [P, G, P], U8)
        a2 = sb("a2", [P, G, 2, P])
        tot = [a2] + [sb(f"tot{s}", [P, G, 2, P // s]) for s in LEVELS[1:]]
        kx = sb("kx", [P, G, P])
        tot_end = sb("tot_end", [P, 2, G])
        kpq = sb("kpq", [P, 2, G, 2, P])
        nm = sb("nm", [P, 2, G, 2, P])
        kxT = sb("kxT", [P, 2, G, P])
        vT = sb("vT", [P, 2, G, P])
        gate = sb("gate", [P, G, P])
        go = sb("go", [P, 2, G, P])
        Tm = sb("Tm", [P, G, P])
        TT = sb("TT", [P, G, P])
        Y = sb("Y", [P, G, P])
        St = sb("St", [P, G, P])
        R = sb("R", [P, G, P])
        Ub = sb("Ub", [P, G, P])
        ot = sb("ot", [P, G, P])
        osq = sb("osq", [P, G, P])
        ors = sb("ors", [P, G, P])
        yo = sb("yo", [P, G, P])
        yx = sb("yx", [P, D])
        ps = lambda n: ctx.enter_context(nc.psum_tensor("d_" + n, [P, G, P], F32))
        psP = [ps("psP0"), ps("psP1")]
        psN = ps("psN")
        psL = ps("psL")
        psB = [ps("psB0"), ps("psB1")]
        psC = [ps("psC0"), ps("psC1")]
        SQ, SUMS, RN = {"k": sq, "q": e3}, {"k": psN, "q": psL}, {"k": rn, "q": e1}
        S = lambda n, lead=0: Signal(ctx, nc, "d_" + n, lead)
        const = S("constants")
        s_h = [S(f"h_loaded{i}") for i in range(2)]
        s_wA, s_wC = S("weights_loaded"), S("out_weights_loaded")
        s_nA = S("decay_rates")
        KQV = "kqv"
        s_proj = {t: S(f"{t}_projected", 2) for t in KQV}
        s_pre = {t: S(f"{t}_copied", 1) for t in KQV}
        s_conv = {t: S(f"{t}_convolved", 1) for t in KQV}
        s_silu = {t: S(f"{t}_silu", 1) for t in KQV}
        s_sq = {t: S(f"{t}_squared", 1) for t in "kq"}
        s_ss = {t: S(f"{t}_square_sum", 1) for t in "kq"}
        s_rn = {t: S(f"{t}_norm", 1) for t in "kq"}
        s_n = {t: S(f"{t}_normed", 1) for t in "kq"}
        s_g, s_xg, s_gl, s_sp, s_a = S("decay_projected", 1), S("decay_biased", 1), S("decay_log", 1), S("softplus", 1), S("decay", 1)
        s_go, s_ge, s_gt = S("gate_projected", 1), S("gate_tanh", 1), S("gate", 1)
        s_vT, s_vTc = S("v_turned", 1), S("v_turned_copied", 1)
        s_kT, s_kTc = S("k_turned", 1), S("k_turned_copied", 1)
        s_L, s_Lc = S("level_product", NL + 1), S("level_kept", 1)
        s_kx, s_kp = S("k_suffix_decayed", 1), S("kq_prefix_decayed", NL + 1)
        s_nm = S("nm_scaled", 1)
        s_T1 = S("inverse_started", 1)
        s_Y, s_Yc, s_Z, s_T, s_Tt, s_TT = S("y_product", 1), S("y_masked", 1), S("z_product", 1), S("t_renewed", 1), S("t_turned", 1), S("t_turned_copied", 1)
        s_Rp, s_R, s_Up, s_U, s_O, s_Sp, s_S = S("r_product", 2), S("r", 2), S("u_product", 1), S("u", 1), S("o_product", 2), S("state_product", 2), S("state", 1)
        s_oc, s_os, s_or, s_y, s_w, s_x = S("o_copied", 1), S("o_square_sum", 1), S("o_norm", 1), S("y_gated", 2), S("out_product", 1), S("x_summed", 1)
        cd, ca, cp = Chain(ctx, nc, "d_dve_chain"), Chain(ctx, nc, "d_act_chain"), Chain(ctx, nc, "d_pool_chain")
        IDX = {"q": 0, "k": 1, "v": 2}
        BANK = {"g": 0, "k": 1, "q": 0, "v": 1, "go": 0}
        W3 = [A["L1_attn_Wq"], A["L1_attn_Wk"], A["L1_attn_Wv"]]
        CW = [A["L1_attn_conv_q_w"], A["L1_attn_conv_k_w"], A["L1_attn_conv_v_w"]]
        NB = NL - 1

        project = ([("a_g",)] + [("a_proj", "k", h) for h in range(G)] + [("a_soft",)] + [("a_proj", "q", h) for h in range(G)]
                   + [("a_proj", "v", h) for h in range(G)] + [("a_go",), ("a_silu",), ("a_sq",)])
        prepare = ([("a_decay",), ("a_ss", "k"), ("a_ss", "q"), ("a_vT",), ("a_gate",), ("a_level0",)]
                   + [("a_level", l) for l in range(NL)] + [("a_end",)])
        use = ([("b_start",)] + [(n, l) for l in range(1, NL) for n in ("b_y", "b_z", "b_t")]
               + [("c_r",), ("c_u",), ("c_o",), ("c_s",), ("c_norm",), ("c_out",)])

        def h_turn(c, b):
            return c * 8 + (16 - 8 * b)

        LENGTH = {"a_proj": 3, "a_silu": 3, "a_level": 2}
        FIRST = ("a_decay",)

        def merged(parts):
            out = []
            for which, items in enumerate(parts):
                length = [LENGTH.get(v[0], 1) for v in items]
                out += [(0.0 if v[0] in FIRST else (sum(length[:i]) + length[i] / 2) / sum(length), which, v) for i, v in enumerate(items)]
            return [(w, v) for _, w, v in sorted(out, key=lambda z: z[:2])]

        def steps(eng, items, chains):
            for ch in chains:
                ch.restart(eng)
            with eng.Fori(0, NQ) as quad:
                def run(c, b, parts):
                    ahead = {id(prepare): 0, id(use): -1, id(project): 1}
                    for which, (name, *rest) in merged(parts):
                        if name in items:
                            d = ahead[id(parts[which])]
                            items[name](quad * C + (c + d), c + d, b if d == 0 else 1 - b, quad, *rest)
                if "start" in items:
                    items["start"](quad)
                run(-1, 1, [project])
                run(0, 0, [prepare, project])
                for ch in chains:
                    ch.restart(eng)
                with eng.Fori(0, C // 2 - 1) as it:
                    run(it * 2 + 1, 1, [prepare, project, use])
                    run(it * 2 + 2, 0, [prepare, project, use])
                    for ch in chains:
                        ch.restart(eng)
                run(C - 1, 1, [prepare, use])
                run(C, 0, [use])
                for ch in chains:
                    ch.restart(eng)

        block = ctx.block(nc)

        @block.sync
        def _(sp):
            with nc.allow_non_contiguous_dma(reason="vectors of a few KB, once"):
                sp.dma_start(dtb[:, :], A["L1_attn_dt_bias"].rearrange("(h p) -> p h", p=P)).then_inc(const.sem, 16)
                sp.dma_start(onw[:, :], A["L1_attn_o_norm_w"].rearrange("(p a) -> p a", a=1)).then_inc(const.sem, 16)
            sp.dma_start(nA[:, :], A["L1_attn_A_log"].rearrange("a b h c -> (a b h c)").partition_broadcast(P)).then_inc(const.sem, 16)
            sp.dma_start(mraw[:, :].rearrange("p (l n) -> p l n", l=NL), A["const_level"]).then_inc(const.sem, 16)
            sp.dma_start(mY[:, :, :], A["const_y"]).then_inc(const.sem, 16)
            sp.dma_start(m1[:, :], A["const_first"]).then_inc(const.sem, 16)
            with sp.Fori(0, NQ) as quad:
                after(sp, K.idle, s_proj["v"].sem, s_proj["v"].of(quad * C - 1))
                for i in range(3):
                    sp.dma_start(w3[:, i, :, :], W3[i].rearrange("(k p) n -> p k n", p=P)[:, :, bass.ds(quad * (G * D1), G * D1)]).then_inc(s_wA.sem, 16)
                after(sp, K.idle, s_go.sem, s_go.of(quad * C - 1))
                for i, w in enumerate((A["L1_attn_Wfb"], A["L1_attn_Wgb"])):
                    sp.dma_start(wfg[:, i, :], w[:, bass.ds(quad * (G * D1), G * D1)]).then_inc(s_wA.sem, 16)
                after(sp, K.idle, s_conv["v"].sem, s_conv["v"].of(quad * C - 1))
                for i in range(3):
                    sp.dma_start(cw[:, i, :, :], CW[i].rearrange("(h p) j -> p h j", p=P)[:, bass.ds(quad * G, G), :]).then_inc(s_wA.sem, 16)
                after(sp, K.idle, s_w.sem, s_w.of(quad * C - 1))
                sp.dma_start(wo[:, :, :], A["L1_attn_Wo"].rearrange("(h p) n -> p h n", p=P)[:, bass.ds(quad * G, G), :]).then_inc(s_wC.sem, 16)
                with sp.Fori(0, C // 2) as it:
                    for b in range(2):
                        after(sp, K.idle, s_go.sem, s_go.of(quad * C + it * 2 + (b - 2)))
                        sp.dma_start(hc[:, b, :, :].rearrange("p k n -> p (k n)"), A["h_scr"][bass.ds(it * 2 + b, 1), :, :].rearrange("a p n -> p (a n)")).then_inc(s_h[b].sem, 16)

        @block.tensor
        def _(pe):
            for s in [*s_proj.values(), *s_ss.values(), s_g, s_go, s_vT, s_kT, s_L, s_Y, s_Z, s_Tt, s_Rp, s_Up, s_O, s_Sp, s_os, s_w]:
                s.start(pe)
            def a_proj(m, c, b, quad, t, h):
                bank = psP[BANK[t]]
                if h == 0:
                    if t == "k":
                        pe.wait_ge(s_pre["v"].sem, s_pre["v"].of(m - 1))
                    if t == "q":
                        pe.wait_ge(s_xg.sem, s_xg.of(m))
                    if t == "v":
                        pe.wait_ge(s_pre["k"].sem, s_pre["k"].of(m))
                for k in range(KC):
                    ins = pe.matmul(bank[:, h, :], w3[:, IDX[t], k, h * D1:(h + 1) * D1], hc[:, b, k, :], start=(k == 0), stop=(k == KC - 1))
                if h == G - 1:
                    ins.then_inc(s_proj[t].sem, 1)

            def a_g(m, c, b, quad):
                pe.wait_ge(s_h[b].sem, quad * (8 * C) + h_turn(c, b))
                pe.wait_ge(s_wA.sem, quad * 128 + 128)
                pe.wait_ge(s_ge.sem, s_ge.of(m - 1))
                for h in range(G):
                    ins = pe.matmul(psP[BANK["g"]][:, h, :], wfg[:, 0, h * D1:(h + 1) * D1], hc[:, b, KC, :], start=True, stop=True)
                ins.then_inc(s_g.sem, 1)

            def a_go(m, c, b, quad):
                pe.wait_ge(s_pre["q"].sem, s_pre["q"].of(m))
                for h in range(G):
                    ins = pe.matmul(psP[BANK["go"]][:, h, :], wfg[:, 1, h * D1:(h + 1) * D1], hc[:, b, KC + 1, :], start=True, stop=True)
                ins.then_inc(s_go.sem, 1)

            def a_ss(m, c, b, quad, t):
                pe.wait_ge(s_sq[t].sem, s_sq[t].of(m))
                if t == "k":
                    pe.wait_ge(s_kTc.sem, s_kTc.of(m - 1))
                else:
                    pe.wait_ge(s_Lc.sem, s_Lc.of(m * (NL + 1) - 1))
                pe.matmul(SUMS[t][:, :, :], ones[:, :], SQ[t][:, :, :], start=True, stop=True).then_inc(s_ss[t].sem, 1)

            def a_vT(m, c, b, quad):
                pe.wait_ge(s_silu["v"].sem, s_silu["v"].of(m))
                pe.wait_ge(s_rn["k"].sem, s_rn["k"].of(m))
                for h in range(G):
                    ins = pe.transpose(psN[:, h, :], qkv[:, IDX["v"], h, :], K.ident[:, :])
                ins.then_inc(s_vT.sem, 1)

            def a_level0(m, c, b, quad):
                pe.wait_ge(s_kx.sem, s_kx.of(m * (NL + 1)))
                pe.wait_ge(s_n["q"].sem, s_n["q"].of(m))
                pe.wait_ge(s_Lc.sem, s_Lc.of(m * (NL + 1) - 1))
                for h in range(G):
                    ins = pe.matmul(psL[:, h, :], kx[:, h, :], qkv[:, 0, h, :], start=True, stop=True)
                ins.then_inc(s_L.sem, 1)

            def a_level(m, c, b, quad, l):
                s = LEVELS[l]
                pe.wait_ge(s_kx.sem, s_kx.of(m * (NL + 1) + l))
                pe.wait_ge(s_kp.sem, s_kp.of(m * (NL + 1) + l))
                pe.wait_ge(s_Lc.sem, s_Lc.of(m * (NL + 1) + l))
                for h in range(G):
                    rhs = kpq[:, b, h, :, :].rearrange("p e (n t s) -> p (e n) t s", t=2, s=s)[:, :, 1, :]
                    ins = pe.matmul(psL[:, h, :], kx[:, h, :], rhs, start=True, stop=True)
                ins.then_inc(s_L.sem, 1)

            def a_end(m, c, b, quad):
                pe.wait_ge(s_kx.sem, s_kx.of(m * (NL + 1) + NL))
                pe.wait_ge(s_vTc.sem, s_vTc.of(m))
                for h in range(G):
                    ins = pe.transpose(psN[:, h, :], kx[:, h, :], K.ident[:, :])
                ins.then_inc(s_kT.sem, 1)

            def turn_T(m, n):
                for h in range(G):
                    ins = pe.transpose(psB[0][:, h, :], (TT if n == 0 else Tm)[:, h, :], K.ident[:, :])
                ins.then_inc(s_Tt.sem, 1)

            def b_start(m, c, b, quad):
                pe.wait_ge(s_T1.sem, s_T1.of(m))
                turn_T(m, 0)

            def b_y(m, c, b, quad, l):
                if l == 1:
                    pe.wait_ge(s_T.sem, s_T.of(m * NL))
                pe.wait_ge(s_TT.sem, s_TT.of(m * NB + (l - 1) - 1))
                for h in range(G):
                    ins = pe.matmul(psB[0][:, h, :], nm[:, b, h, 0, :], Tm[:, h, :], start=True, stop=True)
                ins.then_inc(s_Y.sem, 1)

            def b_z(m, c, b, quad, l):
                pe.wait_ge(s_Yc.sem, s_Yc.of(m * NB + l - 1))
                pe.wait_ge(s_T.sem, s_T.of(m * NL + l - 1))
                for h in range(G):
                    ins = pe.matmul(psB[1][:, h, :], TT[:, h, :], Y[:, h, :], start=True, stop=True)
                ins.then_inc(s_Z.sem, 1)

            def b_t(m, c, b, quad, l):
                pe.wait_ge(s_T.sem, s_T.of(m * NL + l))
                turn_T(m, l)

            def c_r(m, c, b, quad):
                pe.wait_ge(s_kp.sem, s_kp.of(m * (NL + 1) + NL))
                pe.wait_ge(s_S.sem, s_S.of(m - 1))
                pe.wait_ge(s_or.sem, s_or.of(m - 1))
                for h in range(G):
                    ins = pe.matmul(psC[0][:, h, :], kpq[:, b, h, 0, :], St[:, h, :], start=True, stop=True)
                ins.then_inc(s_Rp.sem, 1)

            def c_u(m, c, b, quad):
                pe.wait_ge(s_R.sem, s_R.of(m))
                pe.wait_ge(s_TT.sem, s_TT.of(m * NB + NB - 1))
                pe.wait_ge(s_x.sem, s_x.of(m - 1))
                for h in range(G):
                    ins = pe.matmul(psC[1][:, h, :], TT[:, h, :], R[:, h, :], start=True, stop=True)
                ins.then_inc(s_Up.sem, 1)

            def c_o(m, c, b, quad):
                pe.wait_ge(s_U.sem, s_U.of(m))
                for h in range(G):
                    pe.matmul(psC[1][:, h, :], St[:, h, :], kpq[:, b, h, 1, :], start=True, stop=False)
                    ins = pe.matmul(psC[1][:, h, :], Ub[:, h, :], nm[:, b, h, 1, :], start=False, stop=True)
                ins.then_inc(s_O.sem, 1)

            def c_s(m, c, b, quad):
                pe.wait_ge(s_kTc.sem, s_kTc.of(m))
                for h in range(G):
                    ins = pe.matmul(psC[0][:, h, :], kxT[:, b, h, :], Ub[:, h, :], start=True, stop=True)
                ins.then_inc(s_Sp.sem, 1)

            def c_norm(m, c, b, quad):
                pe.wait_ge(s_oc.sem, s_oc.of(m))
                pe.wait_ge(s_S.sem, s_S.of(m))
                pe.matmul(psC[0][:, :, :], mean[:, :], osq[:, :, :], start=True, stop=True).then_inc(s_os.sem, 1)

            def c_out(m, c, b, quad):
                pe.wait_ge(s_y.sem, s_y.of(m))
                pe.wait_ge(s_wC.sem, quad * 16 + 16)
                flat = psC[1][:, :, :].rearrange("p g n -> p (g n)")
                for h in range(G):
                    ins = pe.matmul(flat, yo[:, h, :], wo[:, h, :], start=(h == 0), stop=(h == G - 1))
                ins.then_inc(s_w.sem, 1)

            steps(pe, {f.__name__: f for f in (a_proj, a_g, a_go, a_ss, a_vT, a_level0, a_level, a_end, b_start, b_y, b_z, b_t, c_r, c_u, c_o, c_s, c_norm, c_out)}, [])

        @block.scalar
        def _(act):
            for s in [*s_pre.values(), *s_silu.values(), *s_sq.values(), *s_rn.values(), s_gl, s_a, s_ge, s_vTc, s_kTc, s_TT, s_oc, s_or]:
                s.start(act)
            load_tables(nc, act, LN_EXP_SET)
            act.wait_ge(const.sem, 96)
            ca.done(act.activation(nA[:, :], nA[:, :], ACT.Exp))
            ca.settle(act)
            act.activation(nA[:, :], nA[:, :], ACT.Copy, scale=-1.0).then_inc(s_nA.sem, 1)

            def a_proj(m, c, b, quad, t, h):
                if h == G - 1:
                    act.wait_ge(s_proj[t].sem, s_proj[t].of(m))
                    act.wait_ge(s_conv[t].sem, s_conv[t].of(m - 1))
                    act.activation(pre[:, b, IDX[t], :, CONV - 1:], psP[BANK[t]][:, :, :], ACT.Copy).then_inc(s_pre[t].sem, 1)

            def a_silu(m, c, b, quad):
                for t in "kq":
                    act.wait_ge(s_conv[t].sem, s_conv[t].of(m))
                    act.wait_ge(s_n[t].sem, s_n[t].of(m - 1))
                    if t == "q":
                        act.wait_ge(s_kp.sem, s_kp.of((m - 1) * (NL + 1)))
                        act.wait_ge(s_L.sem, s_L.of((m - 1) * (NL + 1)))
                    act.activation(qkv[:, IDX[t], :, :], acc[:, IDX[t], :, :], ACT.Silu).then_inc(s_silu[t].sem, 1)
                act.wait_ge(s_go.sem, s_go.of(m))
                act.wait_ge(s_gt.sem, s_gt.of(m - 1))
                act.activation(gate[:, :, :], psP[BANK["go"]][:, :, :], ACT.Tanh, scale=0.5).then_inc(s_ge.sem, 1)
                act.wait_ge(s_conv["v"].sem, s_conv["v"].of(m))
                act.wait_ge(s_vT.sem, s_vT.of(m - 1))
                act.activation(qkv[:, IDX["v"], :, :], acc[:, IDX["v"], :, :], ACT.Silu).then_inc(s_silu["v"].sem, 1)
                load_tables(nc, act, LN_EXP_SET)

            def a_sq(m, c, b, quad):
                act.wait_ge(s_sp.sem, s_sp.of(m))
                for t in "kq":
                    act.wait_ge(s_silu[t].sem, s_silu[t].of(m))
                    act.wait_ge(s_ss[t].sem, s_ss[t].of(m - 1))
                    act.activation(SQ[t][:, :, :], qkv[:, IDX[t], :, :], ACT.Square).then_inc(s_sq[t].sem, 1)

            def a_ss(m, c, b, quad, t):
                act.wait_ge(s_ss[t].sem, s_ss[t].of(m))
                act.wait_ge(s_n[t].sem, s_n[t].of(m - 1))
                ca.done(act.activation(RN[t][:, :, :], SUMS[t][:, :, :], ACT.Ln, bias=K.eps[:, 1:2]))
                ca.settle(act)
                act.activation(RN[t][:, :, :], RN[t][:, :, :], ACT.Exp, scale=-0.5, bias=(K.eps[:, 2:3] if t == "q" else 0.0)).then_inc(s_rn[t].sem, 1)

            def a_vT(m, c, b, quad):
                act.wait_ge(s_vT.sem, s_vT.of(m))
                act.wait_ge(s_R.sem, s_R.of(m - 2))
                act.activation(vT[:, b, :, :], psN[:, :, :], ACT.Copy).then_inc(s_vTc.sem, 1)

            def a_soft(m, c, b, quad):
                act.wait_ge(s_xg.sem, s_xg.of(m))
                act.wait_ge(s_n["q"].sem, s_n["q"].of(m - 1))
                act.wait_ge(s_sp.sem, s_sp.of(m - 1))
                ca.done(act.activation(e2[:, :, :], xg[:, :, :], ACT.Abs))
                ca.settle(act)
                ca.done(act.activation(e1[:, :, :], e2[:, :, :], ACT.Exp, scale=-1.0))
                ca.settle(act)
                act.activation(e2[:, :, :], e1[:, :, :], ACT.Ln, bias=1.0).then_inc(s_gl.sem, 1)

            def a_decay(m, c, b, quad):
                act.wait_ge(s_sp.sem, s_sp.of(m))
                act.wait_ge(s_kp.sem, s_kp.of(m * (NL + 1) - 1))
                act.wait_ge(s_kx.sem, s_kx.of(m * (NL + 1) - 1))
                act.activation(a2[:, :, :, :], bc(xg[:, :, :], 2, [P, G, 2, P]), ACT.Exp).then_inc(s_a.sem, 1)

            def a_end(m, c, b, quad):
                act.wait_ge(s_kT.sem, s_kT.of(m))
                act.wait_ge(s_Sp.sem, s_Sp.of(m - 2))
                act.activation(kxT[:, b, :, :], psN[:, :, :], ACT.Copy).then_inc(s_kTc.sem, 1)

            def b_t(m, c, b, quad, l):
                act.wait_ge(s_Tt.sem, s_Tt.of(m * NL + l))
                act.activation(TT[:, :, :], psB[0][:, :, :], ACT.Copy).then_inc(s_TT.sem, 1)

            def c_o(m, c, b, quad):
                act.wait_ge(s_O.sem, s_O.of(m))
                act.wait_ge(s_y.sem, s_y.of(m - 1))
                act.wait_ge(s_os.sem, s_os.of(m - 1))
                act.activation(ot[:, :, :], psC[1][:, :, :], ACT.Copy)
                act.activation(osq[:, :, :], psC[1][:, :, :], ACT.Square).then_inc(s_oc.sem, 1)

            def c_norm(m, c, b, quad):
                act.wait_ge(s_os.sem, s_os.of(m))
                ca.done(act.activation(ors[:, :, :], psC[0][:, :, :], ACT.Ln, bias=K.eps[:, 1:2]))
                ca.settle(act)
                act.activation(ors[:, :, :], ors[:, :, :], ACT.Exp, scale=-0.5).then_inc(s_or.sem, 1)

            steps(act, {f.__name__: f for f in (a_proj, a_silu, a_sq, a_ss, a_vT, a_soft, a_decay, a_end, b_t, c_o, c_norm)}, [ca])

        @block.gpsimd
        def _(pool):
            for s in (s_kx,):
                s.start(pool)

            def half(ap, s, i):
                return ap.rearrange("p g (n t s) -> p g n t s", t=2, s=s)[:, :, :, i, :]

            def a_ss(m, c, b, quad, t):
                if t == "k":
                    pool.wait_ge(s_rn["k"].sem, s_rn["k"].of(m))
                    pool.wait_ge(s_silu["k"].sem, s_silu["k"].of(m))
                    after(pool, K.idle, s_kT.sem, s_kT.of(m - 1))
                    pool.tensor_tensor(kx[:, :, :], qkv[:, IDX["k"], :, :], rn[:, :, :], ALU.mult).then_inc(s_kx.sem, 1)

            def a_level(m, c, b, quad, l):
                s = LEVELS[l]
                n = P // (2 * s)
                pool.wait_ge(s_L.sem, s_L.of(m * (NL + 1) + l + 1))
                after(pool, K.idle, s_kp.sem, s_kp.of(m * (NL + 1) + l))
                view = half(kx[:, :, :], s, 0)
                whole = tot[l][:, :, 0, :].rearrange("p g (n t) -> p g n t", t=2)[:, :, :, 1]
                pool.tensor_tensor(view, view, bc(whole, 3, [P, G, n, s]), ALU.mult).then_inc(s_kx.sem, 1)

            steps(pool, {f.__name__: f for f in (a_ss, a_level)}, [])

        @block.vector
        def _(dve):
            for s in [*s_conv.values(), *s_n.values(), s_xg, s_sp, s_gt, s_Lc, s_kp, s_nm, s_T1, s_Yc, s_T, s_R, s_U, s_S, s_y, s_x]:
                s.start(dve)
            dve.wait_ge(const.sem, 96)
            dve.memset(ones[:, :], 1.0)
            cd.done(dve.tensor_copy(mT[:, :, :], mraw[:, :].rearrange("p (l n) -> p l n", l=NL)))
            dve.memset(mean[:, :], 1.0 / D1)
            cd.done(dve.tensor_scalar(onw[:, :], onw[:, :], 0.5, None, ALU.mult))
            cd.settle(dve)

            flat = lambda ap: ap.rearrange("p g n -> p (g n)")

            def start(quad):
                dve.wait_ge(s_Sp.sem, s_Sp.of(quad * C - 1))
                dve.wait_ge(s_O.sem, s_O.of(quad * C - 1))
                cd.done(dve.memset(pre[:, 1, :, :, P:], 0.0))
                cd.done(dve.memset(St[:, :, :], 0.0))
                cd.settle(dve)

            def a_proj(m, c, b, quad, t, h):
                if h < G - 1:
                    return
                i = IDX[t]
                if t == "k":
                    dve.wait_ge(s_wA.sem, quad * 128 + 128)
                dve.wait_ge(s_silu[t].sem, s_silu[t].of(m - 1))
                cd.done(dve.tensor_copy(pre[:, b, i, :, 0:CONV - 1], pre[:, 1 - b, i, :, P:]))
                cd.settle(dve)
                dve.wait_ge(s_pre[t].sem, s_pre[t].of(m))
                for j in range(CONV):
                    for g in range(G):
                        src = pre[:, b, i, g, j:j + P]
                        if j == 0:
                            cd.done(dve.tensor_scalar(acc[:, i, g, :], src, cw[:, i, g, 0:1], None, ALU.mult))
                        else:
                            ins = dve.scalar_tensor_tensor(acc[:, i, g, :], src, cw[:, i, g, j:j + 1], acc[:, i, g, :], ALU.mult, ALU.add)
                            if (j, g) == (CONV - 1, G - 1):
                                ins.then_inc(s_conv[t].sem, 1)
                            else:
                                cd.done(ins)
                    if j < CONV - 1:
                        cd.settle(dve)

            def a_g(m, c, b, quad):
                dve.wait_ge(s_g.sem, s_g.of(m))
                dve.wait_ge(s_a.sem, s_a.of(m - 1))
                dve.tensor_tensor(xg[:, :, :], psP[BANK["g"]][:, :, :], bc(dtb[:, bass.ds(quad * G, G)], 2, [P, G, P]), ALU.add).then_inc(s_xg.sem, 1)

            def a_ss(m, c, b, quad, t):
                if t == "q":
                    dve.wait_ge(s_rn[t].sem, s_rn[t].of(m))
                    dve.tensor_tensor(qkv[:, 0, :, :], qkv[:, 0, :, :], RN["q"][:, :, :], ALU.mult).then_inc(s_n["q"].sem, 1)
                else:
                    dve.wait_ge(s_kx.sem, s_kx.of(m * (NL + 1)))
                    dve.sem_inc(s_n["k"].sem, 1)

            def a_soft(m, c, b, quad):
                dve.wait_ge(s_gl.sem, s_gl.of(m))
                dve.wait_ge(s_ss["q"].sem, s_ss["q"].of(m - 1))
                cd.done(dve.tensor_scalar(e3[:, :, :], e1[:, :, :], 1.0 / 3.0, -0.5, ALU.mult, ALU.add))
                cd.done(dve.tensor_scalar(em[:, :, :], e1[:, :, :], 0.01, None, ALU.is_lt))
                cd.settle(dve)
                cd.done(dve.tensor_tensor(e3[:, :, :], e3[:, :, :], e1[:, :, :], ALU.mult))
                cd.settle(dve)
                cd.done(dve.scalar_tensor_tensor(flat(e3[:, :, :]), flat(e3[:, :, :]), 1.0, flat(e1[:, :, :]), ALU.add, ALU.mult))
                cd.settle(dve)
                cd.done(dve.copy_predicated(flat(e2[:, :, :]), flat(em[:, :, :]), flat(e3[:, :, :])))
                cd.settle(dve)
                cd.done(dve.scalar_tensor_tensor(flat(e2[:, :, :]), flat(xg[:, :, :]), 0.0, flat(e2[:, :, :]), ALU.max, ALU.add))
                cd.settle(dve)
                dve.wait_ge(s_nA.sem, 1)
                dve.tensor_tensor(xg[:, :, :], e2[:, :, :], bc(nA[:, bass.ds(quad * G, G)], 2, [P, G, P]), ALU.mult).then_inc(s_sp.sem, 1)

            def a_gate(m, c, b, quad):
                dve.wait_ge(s_ge.sem, s_ge.of(m))
                dve.wait_ge(s_y.sem, s_y.of(m - 2))
                dve.tensor_scalar(go[:, b, :, :], gate[:, :, :], 1.0, onw[:, 0:1], ALU.add, ALU.mult).then_inc(s_gt.sem, 1)

            def a_level0(m, c, b, quad):
                dve.wait_ge(s_a.sem, s_a.of(m))
                dve.wait_ge(s_O.sem, s_O.of(m - 2))
                dve.wait_ge(s_Rp.sem, s_Rp.of(m - 2))
                dve.wait_ge(s_n["q"].sem, s_n["q"].of(m))
                cd.done(dve.tensor_tensor(kpq[:, b, :, 0, :], kx[:, :, :], a2[:, :, 0, :], ALU.mult))
                cd.done(dve.memset(nm[:, b, :, 0, :], 0.0))
                dve.tensor_tensor(kpq[:, b, :, 1, :], qkv[:, 0, :, :], a2[:, :, 1, :], ALU.mult).then_inc(s_kp.sem, 1)
                dve.wait_ge(s_L.sem, s_L.of(m * (NL + 1)))
                dve.tensor_tensor(nm[:, b, :, 1, :], psL[:, :, :], bc(K.ident[:, :], 1, [P, G, P]), ALU.mult).then_inc(s_Lc.sem, 1)

            def a_level(m, c, b, quad, l):
                s = LEVELS[l]
                n = P // (2 * s)
                dve.wait_ge(s_Lc.sem, s_Lc.of(m * (NL + 1) + l))
                after(dve, K.idle, s_L.sem, s_L.of(m * (NL + 1) + l + 1))
                out = nm[:, b, :, :, :].rearrange("p g e (n t s) -> p (g e) n t s", t=2, s=s)[:, :, :, 1, :]
                msk = bc(mT[:, l, :].rearrange("p (n s) -> p n s", s=s), 1, [P, 2 * G, n, s])
                dat = psL[:, :, :].rearrange("p g (e n s) -> p (g e) n s", e=2, s=s)
                dve.copy_predicated(out, msk, dat).then_inc(s_Lc.sem, 1)
                dve.wait_ge(s_kp.sem, s_kp.of(m * (NL + 1) + l))
                old = tot[l][:, :, :, :].rearrange("p g e (n t) -> p (g e) n t", t=2)
                if l + 1 < NL:
                    cd.done(dve.tensor_tensor(tot[l + 1][:, :, :, :].rearrange("p g e n -> p (g e) n"), old[:, :, :, 0], old[:, :, :, 1], ALU.mult))
                else:
                    cd.done(dve.tensor_tensor(tot_end[:, b, :], old[:, ::2, 0, 0], old[:, ::2, 0, 1], ALU.mult))
                view = kpq[:, b, :, :, :].rearrange("p g e (n t s) -> p (g e) n t s", t=2, s=s)[:, :, :, 1, :]
                dve.tensor_tensor(view, view, bc(old[:, :, :, 0], 3, [P, 2 * G, n, s]), ALU.mult).then_inc(s_kp.sem, 1)

            def beta_of(c, quad):
                return bc(K.beta[:, c, bass.ds(quad * G, G)], 2, [P, G, P])

            def a_end(m, c, b, quad):
                dve.wait_ge(s_Lc.sem, s_Lc.of(m * (NL + 1) + NL))
                dve.tensor_tensor(nm[:, b, :, 0, :], nm[:, b, :, 0, :], beta_of(c, quad), ALU.mult).then_inc(s_nm.sem, 1)

            def b_start(m, c, b, quad):
                dve.wait_ge(s_nm.sem, s_nm.of(m))
                dve.wait_ge(s_Up.sem, s_Up.of(m - 1))
                cd.done(dve.tensor_tensor(TT[:, :, :], nm[:, b, :, 0, :], bc(m1[:, :], 1, [P, G, P]), ALU.mult))
                cd.settle(dve)
                dve.tensor_tensor(TT[:, :, :], bc(K.ident[:, :], 1, [P, G, P]), TT[:, :, :], ALU.subtract).then_inc(s_T1.sem, 1)
                dve.wait_ge(s_Tt.sem, s_Tt.of(m * NL))
                dve.tensor_copy(Tm[:, :, :], psB[0][:, :, :]).then_inc(s_T.sem, 1)

            def b_y(m, c, b, quad, l):
                dve.wait_ge(s_Y.sem, s_Y.of(m * NB + l - 1))
                dve.wait_ge(s_Z.sem, s_Z.of(m * NB + l - 2))
                dve.tensor_tensor(Y[:, :, :], psB[0][:, :, :], bc(mY[:, l - 1, :], 1, [P, G, P]), ALU.mult).then_inc(s_Yc.sem, 1)

            def b_z(m, c, b, quad, l):
                dve.wait_ge(s_Z.sem, s_Z.of(m * NB + l - 1))
                dve.wait_ge(s_T.sem, s_T.of(m * NL + l - 1))
                dve.tensor_tensor(Tm[:, :, :], Tm[:, :, :], psB[1][:, :, :], ALU.subtract).then_inc(s_T.sem, 1)

            def c_r(m, c, b, quad):
                dve.wait_ge(s_Rp.sem, s_Rp.of(m))
                dve.wait_ge(s_vTc.sem, s_vTc.of(m))
                dve.tensor_tensor(R[:, :, :], vT[:, b, :, :], psC[0][:, :, :], ALU.subtract).then_inc(s_R.sem, 1)

            def c_u(m, c, b, quad):
                dve.wait_ge(s_Up.sem, s_Up.of(m))
                dve.tensor_tensor(Ub[:, :, :], psC[1][:, :, :], beta_of(c, quad), ALU.mult).then_inc(s_U.sem, 1)

            def c_s(m, c, b, quad):
                dve.wait_ge(s_O.sem, s_O.of(m))
                cd.done(dve.tensor_tensor(St[:, :, :], St[:, :, :], bc(tot_end[:, b, :], 2, [P, G, P]), ALU.mult))
                cd.settle(dve)
                dve.wait_ge(s_Sp.sem, s_Sp.of(m))
                dve.tensor_tensor(St[:, :, :], St[:, :, :], psC[0][:, :, :], ALU.add).then_inc(s_S.sem, 1)

            def c_norm(m, c, b, quad):
                dve.wait_ge(s_oc.sem, s_oc.of(m))
                dve.wait_ge(s_or.sem, s_or.of(m))
                dve.wait_ge(s_gt.sem, s_gt.of(m))
                dve.wait_ge(s_w.sem, s_w.of(m - 1))
                cd.done(dve.tensor_tensor(yo[:, :, :], ot[:, :, :], ors[:, :, :], ALU.mult))
                cd.settle(dve)
                dve.tensor_tensor(yo[:, :, :], yo[:, :, :], go[:, b, :, :], ALU.mult).then_inc(s_y.sem, 1)

            def c_out(m, c, b, quad):
                dve.wait_ge(s_w.sem, s_w.of(m))
                cd.done(dve.tensor_tensor(yx[:, :], psC[1][:, :, :].rearrange("p g n -> p (g n)"), K.gates[:, 1, 0, :], ALU.mult))
                cd.settle(dve)
                dve.tensor_tensor(K.x[:, c, :], K.x[:, c, :], yx[:, :], ALU.add).then_inc(s_x.sem, 1)

            steps(dve, {f.__name__: f for f in (start, a_proj, a_g, a_ss, a_soft, a_gate, a_level0, a_level, a_end, b_start, b_y, b_z, c_r, c_u, c_s, c_norm, c_out)}, [cd])


def phase_ternary(nc, A, K):
    with Phase() as ctx:
        sb = lambda n, s, d=F32: ctx.enter_context(nc.sbuf_tensor("t_" + n, s, d))
        w = sb("w", [P, KC, D])
        var = sb("var", [P, KC, D])
        lo = sb("lo", [P, KC, D])
        wT = sb("wT", [P, KC, D])
        stats = sb("stats", [P, 2, 6])
        mv = sb("mv", [P, 2, 2])
        rstd = sb("rstd", [P, 2, 2])
        xn = sb("xn", [P, 2, D])
        hT = sb("hT", [P, 2, KC * P])
        up = sb("up", [P, 2, KC * P])
        tq = sb("tq", [P, 2, KC * P])
        y = sb("y", [P, 2, D])
        o = sb("o", [P, 2, D])
        ps_w = [ctx.enter_context(nc.psum_tensor(f"t_ps_w{i}", [P, KC, P], F32)) for i in range(2)]
        ps_xT = ctx.enter_context(nc.psum_tensor("t_ps_xT", [P, KC, P], F32))
        ps_y = ctx.enter_context(nc.psum_tensor("t_ps_y", [P, D], F32))
        S = lambda n, lead=0: Signal(ctx, nc, "t_" + n, lead)
        loaded = S("loaded")
        s_wq, s_wt, s_wc = S("weights_made"), S("weights_turned"), S("weights_copied")
        s_mv, s_rstd, s_xn, s_xT, s_hT = S("mean_var"), S("rstd"), S("normed"), S("x_turned", 2), S("h", 1)
        s_tq, s_y, s_o = S("ternary", 2), S("product", 2), S("output", 1)
        s_st = [S(f"stored{i}") for i in range(2)]
        cd, ca = Chain(ctx, nc, "t_dve_chain"), Chain(ctx, nc, "t_act_chain")
        block = ctx.block(nc)

        @block.sync
        def _(sp):
            sp.dma_start(w[:, :, :], A["L1_ffn_weight"].rearrange("(k p) n -> p k n", p=P)).then_inc(loaded.sem, 16)
            sp.dma_start(var[:, :, :], A["L1_ffn_rram_variation"].rearrange("(k p) n -> p k n", p=P)).then_inc(loaded.sem, 16)
            for b in range(2):
                sp.sem_inc(s_st[b].sem, 16)
            with sp.Fori(0, NT // 2) as it:
                for b in range(2):
                    n = it * 2 + b
                    after(sp, K.idle, s_o.sem, s_o.of(n))
                    sp.dma_start(A["out"][0, bass.ds(n * P, P), :], o[:, b, :]).then_inc(s_st[b].sem, 16)
            for b in range(2):
                sp.wait_ge(s_st[b].sem, 16 * (NT // 2) + 16)

        @block.tensor
        def _(pe):
            s_xT.start(pe)
            s_y.start(pe)
            pe.wait_ge(s_wq.sem, 1)
            for k in range(KC):
                if k >= 2:
                    pe.wait_ge(s_wc.sem, k - 1)
                for j in range(KC):
                    ins = pe.transpose(ps_w[k % 2][:, j, :], w[:, j, k * P:(k + 1) * P], K.ident[:, :])
                ins.then_inc(s_wt.sem, 1)
            pe.wait_ge(s_wc.sem, KC)
            with pe.Fori(0, NT // 2) as it:
                for b in range(2):
                    n = it * 2 + b
                    pe.wait_ge(s_xn.sem, s_xn.of(n))
                    pe.wait_ge(s_hT.sem, s_hT.of(n - 1))
                    for k in range(KC):
                        ins = pe.transpose(ps_xT[:, k, :], xn[:, b, k * P:(k + 1) * P], K.ident[:, :])
                    ins.then_inc(s_xT.sem, 1)
                    pe.wait_ge(s_tq.sem, s_tq.of(n))
                    pe.wait_ge(s_o.sem, s_o.of(n - 1))
                    for k in range(KC):
                        ins = pe.matmul(ps_y[:, :], tq[:, b, k * P:(k + 1) * P], wT[:, k, :], start=(k == 0), stop=(k == KC - 1))
                    ins.then_inc(s_y.sem, 1)

        @block.scalar
        def _(act):
            s_hT.start(act)
            for k in range(KC):
                act.wait_ge(s_wt.sem, k + 1)
                act.activation(wT[:, k, :], ps_w[k % 2][:, :, :].rearrange("p k n -> p (k n)"), ACT.Copy, scale=-0.5).then_inc(s_wc.sem, 1)
            load_tables(nc, act, LN_EXP_SET)
            with act.Fori(0, NT // 2) as it:
                for b in range(2):
                    n = it * 2 + b
                    act.wait_ge(s_mv.sem, s_mv.of(n))
                    ca.done(act.activation(rstd[:, b, 0:1], mv[:, b, 1:2], ACT.Ln, bias=K.eps[:, 0:1]))
                    ca.settle(act)
                    act.activation(rstd[:, b, 1:2], rstd[:, b, 0:1], ACT.Exp, scale=-0.5).then_inc(s_rstd.sem, 1)
                    act.wait_ge(s_xT.sem, s_xT.of(n))
                    act.wait_ge(s_tq.sem, s_tq.of(n - 2))
                    for k in range(KC):
                        ins = act.activation(hT[:, b, k * P:(k + 1) * P], ps_xT[:, k, :], ACT.Identity, bias=K.cols[:, 1, 2, k:k + 1], scale=K.cols[:, 1, 3, k:k + 1])
                    ins.then_inc(s_hT.sem, 1)
                ca.restart(act)

        @block.vector
        def _(dve):
            s_tq.start(dve)
            s_o.start(dve)
            dve.wait_ge(loaded.sem, 32)
            cd.done(dve.tensor_scalar(lo[:, :, :], w[:, :, :], -TH_W, SC_W, ALU.is_lt, ALU.mult))
            cd.settle(dve)
            cd.done(dve.tensor_scalar(w[:, :, :], w[:, :, :], TH_W, SC_W, ALU.is_gt, ALU.mult))
            cd.settle(dve)
            cd.done(dve.tensor_tensor(w[:, :, :], w[:, :, :], lo[:, :, :], ALU.subtract))
            cd.settle(dve)
            dve.tensor_tensor(w[:, :, :], w[:, :, :], var[:, :, :], ALU.add).then_inc(s_wq.sem, 1)
            cd.restart(dve)
            with dve.Fori(0, NT // 2) as it:
                for b in range(2):
                    n = it * 2 + b
                    norm_statistics(dve, cd, stats[:, b, :], mv[:, b, :], K.x[:, n, :]).then_inc(s_mv.sem, 1)
                    dve.wait_ge(s_rstd.sem, s_rstd.of(n))
                    dve.wait_ge(s_xT.sem, s_xT.of(n - 2))
                    dve.tensor_scalar(xn[:, b, :], K.x[:, n, :], mv[:, b, 0:1], rstd[:, b, 1:2], ALU.subtract, ALU.mult).then_inc(s_xn.sem, 1)
                    dve.wait_ge(s_hT.sem, s_hT.of(n))
                    cd.done(dve.tensor_scalar(up[:, b, :], hT[:, b, :], TH_X, None, ALU.is_gt))
                    cd.settle(dve)
                    dve.wait_ge(s_y.sem, s_y.of(n - 2))
                    dve.scalar_tensor_tensor(tq[:, b, :], hT[:, b, :], -TH_X, up[:, b, :], ALU.is_lt, ALU.subtract).then_inc(s_tq.sem, 1)
                    dve.wait_ge(s_y.sem, s_y.of(n))
                    cd.done(dve.tensor_tensor(y[:, b, :], ps_y[:, :], K.gates[:, 1, 1, :], ALU.mult))
                    cd.settle(dve)
                    dve.wait_ge(s_st[b].sem, it * 16 + 16)
                    dve.tensor_tensor(o[:, b, :], K.x[:, n, :], y[:, b, :], ALU.add).then_inc(s_o.sem, 1)
                cd.restart(dve)


def build(nc, A):
    K = Held()
    with ExitStack() as ctx:
        K.idle = ctx.enter_context(nc.semaphore("idle"))
        sb = lambda n, s, d=F32: ctx.enter_context(nc.sbuf_tensor("k_" + n, s, d))
        K.x = sb("x", [P, NT, D])
        K.ident = sb("ident", [P, P])
        K.cols = sb("cols", [P, 2, 4, KC])
        K.gates = sb("gates", [P, 2, 2, D])
        K.eps = sb("eps", [P, 3])
        K.zero = sb("zero", [P, 1])
        phase_modulation(nc, A, K)
        phase_qkv(nc, A, K)
        with nc.sbuf_tensor("hT", [P, KC, T], F32) as K.hT:
            with nc.sbuf_tensor("o_all", [P, NT, D], F32) as o_all:
                phase_attention(nc, A, K, o_all)
                phase_attention_out(nc, A, K, o_all)
            phase_mixture(nc, A, K)
        K.beta = sb("beta", [P, NT, H1])
        phase_kda_inputs(nc, A, K)
        phase_kda(nc, A, K)
        phase_ternary(nc, A, K)


_INS = ['L0_attn_x', 'L0_attn_Wqkv', 'L0_attn_Wo', 'L0_ffn_Wr', 'L0_ffn_Wsg', 'L0_c', 'L0_wmod',
        'L1_attn_Wq', 'L1_attn_Wk', 'L1_attn_Wv', 'L1_attn_conv_q_w', 'L1_attn_conv_k_w', 'L1_attn_conv_v_w', 'L1_attn_A_log',
        'L1_attn_Wfa', 'L1_attn_Wfb', 'L1_attn_dt_bias', 'L1_attn_Wb', 'L1_attn_Wga', 'L1_attn_Wgb', 'L1_attn_o_norm_w', 'L1_attn_Wo',
        'L1_ffn_weight', 'L1_ffn_rram_variation', 'L1_c', 'L1_wmod']


def constants():
    i = np.arange(D0 // 2, dtype=np.float32)
    inv = (np.float32(1.0) / np.float32(10000.0) ** (np.float32(2.0) * i / np.float32(D0))).astype(np.float32)
    th = np.outer(np.arange(T, dtype=np.float32), inv).astype(np.float32)
    rope = np.stack([np.cos(th), np.sin(th)], axis=1).astype(np.float32)
    ident = np.eye(P, dtype=np.float32)
    k, q = np.arange(P)[:, None], np.arange(P)[None, :]
    causal = np.where(k > q, -3e38, 0.0).astype(np.float32)
    level = np.zeros((P, len(LEVELS), P // 2), np.float32)
    y = np.zeros((P, len(LEVELS) - 1, P), np.float32)
    for l, s in enumerate(LEVELS):
        r = np.arange(P)
        late = r[(r // s) % 2 == 1]
        pair = (r[:, None] // (2 * s) == r[None, :] // (2 * s)) & ((r[:, None] // s) % 2 == 0) & ((r[None, :] // s) % 2 == 1)
        level[:, l, :] = pair[:, late]
        if l:
            y[:, l - 1, :] = pair.T
        else:
            first = pair.astype(np.float32)
    return {"const_level": level, "const_y": y, "const_first": first, "const_rope": rope, "const_ident": ident, "const_causal": causal, "const_before": (np.arange(E)[None, :] < np.arange(E)[:, None]).astype(np.float32)}


def kernel(**inputs):
    import numpy as _np
    import concourse.bacc as _bacc
    from concourse import mybir as _mybir
    from concourse.bass_utils import run_bass_kernel_spmd as _run

    nc = _bacc.Bacc("TRN2", target_bir_lowering=False, num_devices=1)
    arrays = {name: _np.ascontiguousarray(inputs[name]) for name in _INS}
    arrays.update(constants())
    cut = (UNITS - E)
    arrays["Wg_all"] = _np.concatenate([inputs["L0_ffn_Wg"], _np.transpose(_np.reshape(inputs["L0_ffn_Sg"], (D, cut, F)), (1, 0, 2))])
    arrays["Wu_all"] = _np.concatenate([inputs["L0_ffn_Wu"], _np.transpose(_np.reshape(inputs["L0_ffn_Su"], (D, cut, F)), (1, 0, 2))])
    arrays["Wd_all"] = _np.concatenate([inputs["L0_ffn_Wd"], _np.reshape(inputs["L0_ffn_Sd"], (cut, F, D))])
    A, feed = {}, {}
    for name, a in arrays.items():
        feed[f"in_{name}"] = a
        A[name] = nc.dram_tensor(f"in_{name}", a.shape, _mybir.dt.from_np(a.dtype), kind="ExternalInput").ap()
    for name, shape in (("mod_scr", (2, 4 * D)), ("v_scr", (T, D)), ("ct_scr", (UNITS, T)), ("h_scr", (NT, P, (KC + 2) * P))):
        A[name] = nc.dram_tensor(name, shape, F32).ap()
    A["qk_scr"] = nc.dram_tensor("qk_scr", (3, 2 * D, T), BF16).ap()
    A["out"] = nc.dram_tensor("out_0", (1, T, D), F32, kind="ExternalOutput").ap()
    build(nc, A)
    r = _run(nc, [feed], core_ids=[0])
    return r.results[0]["out_0"]
```
